# Optimizing a Trainium2 kernel written in Bass

```python
import numpy as np
import jax
import jax.numpy as jnp

def _softmax(x, axis=-1):
    return jax.nn.softmax(x, axis=axis)

def _gelu(x):
    return jax.nn.gelu(x, approximate=True)

def _silu(x):
    return jax.nn.silu(x)

def _sigmoid(x):
    return jax.nn.sigmoid(x)

def _layernorm(x, axis=-1, eps=1e-05):
    m = jnp.mean(x, axis=axis, keepdims=True)
    v = jnp.var(x, axis=axis, keepdims=True)
    return (x - m) / jnp.sqrt(v + eps)

def _scatter_add(tgt, idx, src, axis=0):
    return tgt.at[idx].add(src)

def _segment_sum(src, seg, n):
    return jax.ops.segment_sum(src, seg, n)
kernel_name = 'mk_gnn_resnorm_d1_gnn_r8_220b8f'

def setup_inputs(seed: int=0):
    np.random.seed(seed)
    _w = jnp.asarray

    def _rec_inputs():
        import jax
        import jax.numpy as jnp
        _gk = jax.random.key(seed)
        x = -0.0005121 + 1.001 * jax.random.normal(jax.random.fold_in(_gk, 1), (6250, 64), jnp.float32)
        _s = jax.random.randint(jax.random.fold_in(_gk, 2), (100000,), 0, 6250, jnp.int32)
        _d = jax.random.randint(jax.random.fold_in(_gk, 3), (100000,), 0, 6250, jnp.int32)
        _loop = jnp.arange(6250, dtype=jnp.int32)
        src = jnp.concatenate([_s, _d, _loop])
        dst = jnp.concatenate([_d, _s, _loop])
        _o = jnp.argsort(dst, stable=True)
        src = src[_o]
        dst = dst[_o]
        edge_attr_64 = -8.16379e-05 + 0.999858 * jax.random.normal(jax.random.fold_in(_gk, 11), (206250, 64), jnp.float32)
        return (x, src, dst, edge_attr_64)
    x, src, dst, edge_attr_64 = _rec_inputs()

    def _L0_gnn_setup():
        import jax, jax.numpy as jnp
        import numpy as np
        N = 6250
        EG = 200000
        IN = 64
        OUT = 64
        H = 4
        D = OUT // H
        key = jax.random.key(seed)
        ks = jax.random.split(key, 12)
        s = 1.0 / np.sqrt(IN)
        return {'x': jax.random.normal(ks[0], (N, IN), jnp.float32), 'edge_attr': jax.random.normal(ks[1], (EG, IN), jnp.float32), 'edge_index': jax.random.randint(ks[2], (2, EG), 0, N, jnp.int32), 'Wq': jax.random.uniform(ks[3], (OUT, IN), jnp.float32, -s, s), 'bq': jax.random.uniform(ks[4], (OUT,), jnp.float32, -s, s), 'Wk': jax.random.uniform(ks[5], (OUT, IN), jnp.float32, -s, s), 'bk': jax.random.uniform(ks[6], (OUT,), jnp.float32, -s, s), 'We': jax.random.uniform(ks[7], (OUT, IN), jnp.float32, -s, s), 'be': jax.random.uniform(ks[8], (OUT,), jnp.float32, -s, s), 'Wv': jax.random.uniform(ks[9], (OUT, IN), jnp.float32, -s, s), 'bv': jax.random.uniform(ks[10], (OUT,), jnp.float32, -s, s)}
    _L0_gnn_all = _L0_gnn_setup()
    _L0_gnn_in = {k: v for k, v in _L0_gnn_all.items() if k in ('Wq', 'bq', 'Wk', 'bk', 'We', 'be', 'Wv', 'bv')}
    del _L0_gnn_all
    return {'x': x, 'src': src, 'dst': dst, 'edge_attr_64': edge_attr_64, 'L0_gnn_Wq': _L0_gnn_in['Wq'], 'L0_gnn_bq': _L0_gnn_in['bq'], 'L0_gnn_Wk': _L0_gnn_in['Wk'], 'L0_gnn_bk': _L0_gnn_in['bk'], 'L0_gnn_We': _L0_gnn_in['We'], 'L0_gnn_be': _L0_gnn_in['be'], 'L0_gnn_Wv': _L0_gnn_in['Wv'], 'L0_gnn_bv': _L0_gnn_in['bv']}

def reference(x, src, dst, edge_attr_64, L0_gnn_Wq, L0_gnn_bq, L0_gnn_Wk, L0_gnn_bk, L0_gnn_We, L0_gnn_be, L0_gnn_Wv, L0_gnn_bv):
    import jax
    import jax.numpy as jnp

    def _L0_gnn_ref(x, edge_attr, edge_index, Wq, bq, Wk, bk, We, be, Wv, bv):
        import jax, jax.numpy as jnp
        import numpy as np
        N = 6250
        EG = 200000
        IN = 64
        OUT = 64
        H = 4
        D = OUT // H
        n = x.shape[0]
        Qh = (x @ Wq.T + bq).reshape(n, H, D)
        Kh = (x @ Wk.T + bk).reshape(n, H, D)
        Vh = (x @ Wv.T + bv).reshape(n, H, D)
        Ee = (edge_attr @ We.T + be).reshape(-1, H, D)
        src = edge_index[0]
        dst = edge_index[1]
        score = (Kh[src] * Qh[dst] * (1.0 / np.sqrt(D)) * Ee).sum(-1)
        score = jnp.exp(jnp.clip(score, -5.0, 5.0))
        msg = Vh[src] * score[..., None]
        wV = jax.ops.segment_sum(msg, dst, num_segments=n)
        return wV.reshape(n, H * D)
    edge_index = jnp.stack([src, dst])
    x = _layernorm(x + _L0_gnn_ref(x, edge_attr_64, edge_index, L0_gnn_Wq, L0_gnn_bq, L0_gnn_Wk, L0_gnn_bk, L0_gnn_We, L0_gnn_be, L0_gnn_Wv, L0_gnn_bv), axis=-1)
    return x

_drawn_inputs = setup_inputs


def setup_inputs(seed=0):
    import zlib

    import numpy as np

    out = dict(_drawn_inputs(seed))
    spreads = {}
    factors = {'L0_gnn_bq': 2.919}
    for name, (base, spread) in spreads.items():
        noise = np.random.default_rng([zlib.crc32(name.encode()), seed]).standard_normal(out[name].shape)
        drawn = base * np.exp(spread * noise) if base else spread * noise
        out[name] = jnp.asarray(drawn.astype(out[name].dtype))
    for name, factor in factors.items():
        out[name] = (out[name] * factor).astype(out[name].dtype)
    return out
```

```python
from contextlib import ExitStack

import concourse.bass as bass
from concourse import mybir

F32 = mybir.dt.float32
BF16 = mybir.dt.bfloat16
I32 = mybir.dt.int32
ALU = mybir.AluOpType
ACT = mybir.ActivationFunctionType
AX_X = mybir.AxisListType.X
ds = bass.ds

P = 128
N = 6250
E = 206250
F = 64
H = 4
D = F // H
CLIP = 5.0
EPS = 1e-5

W = 64
T = 8
PAIRS = T // 2
TILES = -(-E // P)
G = -(-TILES // T)
LAST_PAIRS = (TILES - (G - 1) * T + 1) // 2
SLOTS = 4
ITERS = (G - 1) // SLOTS
NT = -(-N // P)
NPAD = NT * P
PASSES = -(-NPAD // W)
BASE_MAX = NPAD - W
CH = 7
CHUNKS = NT // CH
GPAD = (ITERS + 2) * SLOTS
assert CHUNKS * CH == NT and PASSES * W == NPAD and N < NPAD
assert ITERS * SLOTS < G <= GPAD and TILES % 2 == 0


def gnn_kernel(nc, xT, x_nodes, w_kvq, We_t, be_row, src_tab, dst_tab, dst_first, attr, out):
    ctx = ExitStack()
    with ctx:
        def sb(name, shape, dt):
            return ctx.enter_context(nc.sbuf_tensor(name, shape, dt))

        def ps(name, shape, dt):
            return ctx.enter_context(nc.psum_tensor(name, shape, dt))

        def sem(name):
            return ctx.enter_context(nc.semaphore(name))

        kv_table = nc.dram_tensor("kv_table", [NPAD, 2 * F], F32, kind="Internal").ap()
        q_table = nc.dram_tensor("q_table", [NPAD, 3 * F], BF16, kind="Internal").ap()

        xT_sb = sb("xT_sb", [F + 1, NPAD], F32)
        w_sb = sb("w_sb", [F + 1, 3 * F], F32)
        kv_stage = sb("kv_stage", [P, NT, 2 * F], F32)
        q_stage = sb("q_stage", [P, NT, 3, F], BF16)
        q_rest = sb("q_rest", [P, 2, CH, F], F32)
        x_sb = sb("x_sb", [P, NT, F], F32)
        acc = sb("acc", [P, NPAD], F32)
        src_sb = sb("src_sb", [P, GPAD * T], I32)
        dst_i = sb("dst_i", [P, G, T], I32)
        dst_rel = sb("dst_rel", [P, G, T], F32)
        first_i = sb("first_i", [P, G], I32)
        base_f = sb("base_f", [P, G], F32)
        base_i = sb("base_i", [P, G], I32)
        limits = sb("limits", [P, 2], F32)
        limits_all = sb("limits_all", [P, 2], F32)
        flags = sb("flags", [P, 4], F32)
        passes_i = sb("passes_i", [P, 1], I32)
        iota_i = sb("iota_i", [P, W], I32)
        ident = sb("ident", [P, P], F32)
        fold = sb("fold", [P, F], F32)
        ones = sb("ones", [P, P], F32)
        be_sb = sb("be_sb", [P, T, F], F32)
        we_sb = sb("we_sb", [P, 2 * F], F32)
        idx = sb("idx", [P, SLOTS, T], I32)
        kv = sb("kv", [P, SLOTS, T, 2 * F], F32)
        attr_sb = sb("attr_sb", [P, SLOTS, PAIRS * P], F32)
        q_win = sb("q_win", [P, SLOTS, 2, 3, F], BF16)
        onehot = sb("onehot", [P, 2, T, W], F32)
        onehot_t = sb("onehot_t", [P, PAIRS, P], BF16)
        kq = sb("kq", [P, T, F], F32)
        kqe = sb("kqe", [P, T, F], F32)
        score = sb("score", [P, T * H], F32)
        score_c = sb("score_c", [P, T * H], F32)
        msg = sb("msg", [P, 2, T, F], F32)
        h_sb = kv_stage[:, :, 0:F]
        c_sb = kv_stage[:, :, F:2 * F]
        sq_sb = sb("sq_sb", [P, 2, CH, F], F32)
        y_sb = sb("y_sb", [P, NT, F], F32)
        mean = sb("mean", [P, NT], F32)
        neg_mean = sb("neg_mean", [P, NT], F32)
        var = sb("var", [P, NT], F32)
        var_e = sb("var_e", [P, NT], F32)
        std = sb("std", [P, NT], F32)
        rstd = sb("rstd", [P, NT], F32)

        ee_ps = [ps(f"ee_ps{i}", [P, T, F], F32) for i in range(2)]
        qe_ps = [ps(f"qe_ps{i}", [P, T, F], F32) for i in range(2)]
        oht_ps = ps("oht_ps", [P, PAIRS, P], F32)
        sum_ps = ps("sum_ps", [P, 4, P], F32)
        iota_bank = ps("iota_bank", [P, 512], F32)
        exp_bank = ps("exp_bank", [P, 512], F32)
        iota_ps = iota_bank[:, 0:W]
        p_ps = exp_bank[:, 0:T * H]
        kv_banks = [ee_ps[0], ee_ps[1], qe_ps[0], qe_ps[1]]
        q_banks = [oht_ps, sum_ps]

        def bank(b, n):
            return b[:].rearrange("p a b -> p (a b)")[:, 0:n]

        w_loaded = sem("w_loaded")
        x_loaded = [sem(f"x_loaded{i}") for i in range(CHUNKS)]
        dst_loaded = sem("dst_loaded")
        src_loaded = sem("src_loaded")
        we_loaded = sem("we_loaded")
        xn_loaded = sem("xn_loaded")
        consts_zeroed = sem("consts_zeroed")
        ident_zeroed = sem("ident_zeroed")
        ident_set = sem("ident_set")
        iota_set = sem("iota_set")
        wq_scaled = sem("wq_scaled")
        kv_computed = sem("kv_computed")
        kv_staged = sem("kv_staged")
        q_computed = sem("q_computed")
        q_part0 = sem("q_part0")
        q_rested = sem("q_rested")
        q_part1 = sem("q_part1")
        q_staged = sem("q_staged")
        kv_stored = sem("kv_stored")
        q_stored = sem("q_stored")
        dst_step = sem("dst_step")
        limits_set = sem("limits_set")
        limits_joined = sem("limits_joined")

        wv_turned = sem("wv_turned")
        h_added = sem("h_added")
        mean_step = sem("mean_step")
        centered = sem("centered")
        squared = sem("squared")
        var_summed = sem("var_summed")
        std_step = sem("std_step")
        std_rooted = sem("std_rooted")
        y_done = sem("y_done")
        y_stored = sem("y_stored")

        attr_loaded = [sem(f"attr_loaded{j}") for j in range(SLOTS)]
        q_loaded = [sem(f"q_loaded{j}") for j in range(SLOTS)]
        kv_gathered = [sem(f"kv_gathered{j}") for j in range(SLOTS)]
        slot_ready = sem("slot_ready")
        gathers_begun = sem("gathers_begun")
        onehot_made = sem("onehot_made")
        ee_made = sem("ee_made")
        onehot_turned = sem("onehot_turned")
        onehot_t_made = sem("onehot_t_made")
        qe_made = sem("qe_made")
        kq_made = sem("kq_made")
        kqe_made = sem("kqe_made")
        score_summed = sem("score_summed")
        score_clipped = sem("score_clipped")
        exp_made = sem("exp_made")
        msg_made = sem("msg_made")
        sums_made = sem("sums_made")
        acc_added = sem("acc_added")
        window_moved = sem("window_moved")
        pass_sems = range(attr_loaded[0].num, window_moved.num + 1)
        assert len(pass_sems) == 3 * SLOTS + 16

        with nc.Block() as block:
            @block.sync
            def _(sp):
                sp.dma_start(w_sb[:, :], w_kvq).then_inc(w_loaded, 16)
                for c in range(CHUNKS):
                    cols = slice(c * CH * P, (c + 1) * CH * P)
                    sp.dma_start(xT_sb[:, cols], xT[:, cols]).then_inc(x_loaded[c], 16)
                sp.dma_start(dst_i[:, :, :], dst_tab).then_inc(dst_loaded, 16)
                sp.dma_start(first_i[:, :], dst_first).then_inc(dst_loaded, 16)
                sp.dma_start(src_sb[:, :], src_tab).then_inc(src_loaded, 16)
                sp.wait_ge(consts_zeroed, 4)
                sp.dma_start(we_sb[0:F, 0:F], We_t).then_inc(we_loaded, 16)
                sp.dma_start(we_sb[F:2 * F, F:2 * F], We_t).then_inc(we_loaded, 16)
                for t in range(T):
                    sp.dma_start(be_sb[0:1, t, :], be_row).then_inc(we_loaded, 16)
                sp.dma_start(x_sb[:, :, :], x_nodes).then_inc(xn_loaded, 16)
                kv_rows = kv_table.rearrange("(p t) f -> p t f", t=NT)
                q_rows = q_table.rearrange("(p t) (s f) -> p t s f", t=NT, s=3)
                for c in range(CHUNKS):
                    sp.wait_ge(kv_staged, 2 * (c + 1))
                    sp.dma_start(kv_rows[:, c * CH:(c + 1) * CH, :],
                                 kv_stage[:, c * CH:(c + 1) * CH, :]).then_inc(kv_stored, 16)
                for c in range(CHUNKS):
                    sp.wait_ge(q_staged, c + 1)
                    sp.dma_start(q_rows[:, c * CH:(c + 1) * CH, :, :],
                                 q_stage[:, c * CH:(c + 1) * CH, :, :]).then_inc(q_stored, 16)
                sp.wait_ge(src_loaded, 16)
                sp.wait_ge(we_loaded, 16 * (2 + T))
                sp.wait_ge(xn_loaded, 16)
                sp.wait_ge(kv_stored, 16 * CHUNKS)
                sp.wait_ge(q_stored, 16 * CHUNKS)

            @block.gpsimd
            def _(pool):
                pool.memset(we_sb[:, :], 0.0).then_inc(consts_zeroed, 1)
                pool.memset(be_sb[:, :, :], 0.0).then_inc(consts_zeroed, 1)
                pool.memset(q_win[:, :, :, :, :], 0.0).then_inc(consts_zeroed, 1)
                pool.memset(ones[:, :], 1.0).then_inc(consts_zeroed, 1)
                pool.memset(ident[:, :], 0.0).then_inc(ident_zeroed, 1)
                pool.wait_ge(ident_zeroed, 1)
                pool.affine_select(out=ident[:, :], in_=ident[:, :], compare_op=ALU.not_equal, fill=1.0,
                                   base=0, pattern=[[-1, P]], channel_multiplier=1).then_inc(ident_set, 1)
                pool.iota(iota_i[:, :], pattern=[[1, W]], base=0, channel_multiplier=0).then_inc(iota_set, 1)
                pool.memset(acc[:, :], 0.0).then_inc(consts_zeroed, 1)
                pool.wait_ge(limits_set, 2)
                pool.partition_all_reduce(limits_all[:, :], limits[:, :], P,
                                          bass.bass_isa.ReduceOp.max).then_inc(limits_joined, 1)

            @block.tensor
            def _(pe):
                pe.wait_ge(w_loaded, 16)
                for c in range(CHUNKS):
                    pe.wait_ge(x_loaded[c], 16)
                    if c >= 2:
                        pe.wait_ge(kv_staged, 2 * (c - 1))
                    for k in range(CH):
                        t = c * CH + k
                        b = kv_banks[2 * (c % 2) + k // 4]
                        mm = pe.matmul(bank(b, 512)[:, (k % 4) * 2 * F:(k % 4 + 1) * 2 * F],
                                       xT_sb[:, t * P:(t + 1) * P], w_sb[:, 0:2 * F], start=True, stop=True)
                        if k == 3 or k == CH - 1:
                            mm.then_inc(kv_computed, 1)
                pe.wait_ge(wq_scaled, 1)
                for c in range(CHUNKS):
                    if c >= 2:
                        pe.wait_ge(q_rested, c - 1)
                    for k in range(CH):
                        t = c * CH + k
                        mm = pe.matmul(bank(q_banks[c % 2], 512)[:, k * F:(k + 1) * F],
                                       xT_sb[:, t * P:(t + 1) * P], w_sb[:, 2 * F:3 * F], start=True, stop=True)
                    mm.then_inc(q_computed, 1)

            @block.scalar
            def _(act):
                for c in range(CHUNKS):
                    for half, n in ((0, 4), (1, CH - 4)):
                        act.wait_ge(kv_computed, 2 * c + half + 1)
                        a = c * CH + 4 * half
                        act.copy(kv_stage[:, a:a + n, :],
                                 bank(kv_banks[2 * (c % 2) + half], n * 2 * F)
                                 .rearrange("p (t f) -> p t f", f=2 * F)).then_inc(kv_staged, 1)
                for c in range(CHUNKS):
                    cols = slice(c * CH, (c + 1) * CH)
                    act.wait_ge(q_computed, c + 1)
                    act.copy(q_stage[:, cols, 0, :], bank(q_banks[c % 2], CH * F)
                             .rearrange("p (t f) -> p t f", f=F)).then_inc(q_part0, 1)
                    act.wait_ge(q_rested, c + 1)
                    act.copy(q_stage[:, cols, 1, :], q_rest[:, c % 2, :, :]).then_inc(q_part1, 1)

            @block.vector
            def _(dve):
                dve.wait_ge(w_loaded, 16)
                dve.tensor_scalar(w_sb[:, 2 * F:3 * F], w_sb[:, 2 * F:3 * F], float(D) ** -0.5, None,
                                  ALU.mult).then_inc(wq_scaled, 1)
                dve.wait_ge(iota_set, 1)
                dve.tensor_copy(iota_ps, iota_i[:, :]).then_inc(dst_step, 1)
                dve.wait_ge(ident_set, 1)
                dve.tensor_tensor(fold[:, :], ident[:, 0:F], ident[:, F:2 * F], ALU.add).then_inc(dst_step, 1)
                dve.wait_ge(dst_loaded, 32)
                dve.tensor_scalar(base_f[:, :], first_i[:, :], float(BASE_MAX), None, ALU.min).then_inc(dst_step, 1)
                dve.wait_ge(dst_step, 3)
                base_b = base_f[:, :].unsqueeze(2).to_broadcast([P, G, T])
                dve.tensor_tensor(dst_rel[:, :, :], dst_i[:, :, :], base_b, ALU.subtract).then_inc(dst_step, 1)
                dve.wait_ge(dst_step, 4)
                rel = dst_rel[:, :, :].rearrange("p g t -> p (g t)")
                dve.tensor_reduce(limits[:, 0:1], rel, AX_X, ALU.max).then_inc(limits_set, 1)
                dve.tensor_reduce(limits[:, 1:2], rel, AX_X, ALU.min, negate=True).then_inc(limits_set, 1)
                dve.wait_ge(limits_joined, 1)
                dve.tensor_scalar(flags[:, 0:1], limits_all[:, 0:1], float(W - 1), None, ALU.is_gt)\
                   .then_inc(dst_step, 1)
                dve.tensor_scalar(flags[:, 1:2], limits_all[:, 1:2], 0.0, None, ALU.is_gt).then_inc(dst_step, 1)
                dve.wait_ge(dst_step, 6)
                dve.tensor_tensor(flags[:, 2:3], flags[:, 0:1], flags[:, 1:2], ALU.max).then_inc(dst_step, 1)
                dve.wait_ge(dst_step, 7)
                dve.tensor_scalar(flags[:, 3:4], flags[:, 2:3], -1.0, 1.0, ALU.mult, ALU.add).then_inc(dst_step, 1)
                dve.tensor_scalar(passes_i[:, :], flags[:, 2:3], float(PASSES - 1), 1.0, ALU.mult, ALU.add)\
                   .then_inc(dst_step, 1)
                dve.wait_ge(dst_step, 9)
                dve.tensor_scalar(base_i[:, :], base_f[:, :], flags[:, 3:4], None, ALU.mult).then_inc(dst_step, 1)
                dve.scalar_tensor_tensor(out=dst_rel[:, :, :], in0=base_b, scalar=flags[:, 2:3],
                                         in1=dst_rel[:, :, :], op0=ALU.mult, op1=ALU.add).then_inc(dst_step, 1)
                dve.wait_ge(dst_step, 11)
                for c in range(CHUNKS):
                    cols = slice(c * CH, (c + 1) * CH)
                    dve.wait_ge(q_part0, c + 1)
                    dve.tensor_tensor(q_rest[:, c % 2, :, :],
                                      bank(q_banks[c % 2], CH * F).rearrange("p (t f) -> p t f", f=F),
                                      q_stage[:, cols, 0, :], ALU.subtract).then_inc(q_rested, 1)
                    dve.wait_ge(q_part1, c + 1)
                    dve.tensor_tensor(q_stage[:, cols, 2, :], q_rest[:, c % 2, :, :],
                                      q_stage[:, cols, 1, :], ALU.subtract).then_inc(q_staged, 1)

        passes = nc.values_load(passes_i[0:1, 0:1], min_val=1, max_val=PASSES)

        with nc.Fori(0, passes):
            with nc.Block() as block:
                def pairs_of(g):
                    return LAST_PAIRS if isinstance(g, int) and g == G - 1 else PAIRS

                @block.sync
                def _(sp):
                    def load(g, slot):
                        n = pairs_of(g) * P
                        sp.dma_start(attr_sb[:, slot, 0:n], attr[ds(g, 1), :, 0:n].rearrange("o p n -> (o p) n"))\
                          .then_inc(attr_loaded[slot], 16)
                        base = sp.value_load(base_i[0:1, ds(g, 1)], min_val=0, max_val=BASE_MAX)
                        rows = q_table[ds(base, W), :].rearrange("n (s f) -> n s f", s=3)
                        sp.dma_start(q_win[0:W, slot, 0, :, :], rows).then_inc(q_loaded[slot], 16)
                        sp.dma_start(q_win[W:2 * W, slot, 1, :, :], rows).then_inc(q_loaded[slot], 16)

                    def load_next(g, slot):
                        sp.wait_ge(ee_made, g - SLOTS + 1)
                        sp.wait_ge(qe_made, g - SLOTS + 1)
                        load(g, slot)

                    for j in range(SLOTS):
                        load(j, j)
                    with sp.Fori(0, ITERS - 1) as i:
                        for j in range(SLOTS):
                            load_next(i * SLOTS + (SLOTS + j), j)
                    for g in range(ITERS * SLOTS, G):
                        load_next(g, g % SLOTS)

                @block.gpsimd
                def _(pool):
                    def gather(g, slot):
                        pool.wait_ge(slot_ready, g + 1)
                        pool.sem_inc(gathers_begun, 1)
                        for t in range(2 * pairs_of(g)):
                            pool.indirect_dma_start(
                                out=kv[:, slot, t, :], out_offset=None, in_=kv_table,
                                in_offset=bass.IndirectOffsetOnAxis(ap=idx[:, slot, t:t + 1], axis=0))\
                                .then_inc(kv_gathered[slot], 16)

                    with pool.Fori(0, ITERS) as i:
                        for j in range(SLOTS):
                            gather(i * SLOTS + j, j)
                    for g in range(ITERS * SLOTS, G):
                        gather(g, g % SLOTS)

                @block.tensor
                def _(pe):
                    def edges_and_onehot(g, slot, turn):
                        n = pairs_of(g)
                        pe.wait_ge(attr_loaded[slot], 16 * (turn + 1))
                        ee = bank(ee_ps[slot % 2], n * P)
                        pe.matmul(ee, ones[:, :], be_sb[:, 0:2 * n, :].rearrange("p t f -> p (t f)"),
                                  start=True, stop=False)
                        for k in range(n):
                            mm = pe.matmul(ee[:, k * P:(k + 1) * P], attr_sb[:, slot, k * P:(k + 1) * P],
                                           we_sb[:, :], start=False, stop=(k == n - 1))
                        mm.then_inc(ee_made, 1)
                        pe.wait_ge(onehot_made, g + 1)
                        for k in range(n):
                            mm = pe.transpose(oht_ps[:, k, :],
                                              onehot[:, slot % 2, 2 * k:2 * k + 2, :].rearrange("p t w -> p (t w)"),
                                              ident[:, :])
                        mm.then_inc(onehot_turned, 1)

                    def fetch_q(g, slot, turn):
                        n = pairs_of(g)
                        pe.wait_ge(q_loaded[slot], 32 * (turn + 1))
                        pe.wait_ge(onehot_t_made, g + 1)
                        for k in range(n):
                            for s in range(3):
                                mm = pe.matmul(bank(qe_ps[slot % 2], n * P)[:, k * P:(k + 1) * P],
                                               onehot_t[:, k, :], q_win[:, slot, :, s, :],
                                               start=(s == 0), stop=(s == 2))
                        mm.then_inc(qe_made, 1)

                    def sum_messages(g, slot):
                        n = pairs_of(g)
                        pe.wait_ge(msg_made, g + 1)
                        for k in range(n):
                            mm = pe.matmul(sum_ps[:, slot % 2, :],
                                           msg[:, slot % 2, 2 * k:2 * k + 2, :].rearrange("p t f -> p (t f)"),
                                           onehot[:, slot % 2, 2 * k:2 * k + 2, :].rearrange("p t w -> p (t w)"),
                                           start=(k == 0), stop=(k == n - 1))
                        mm.then_inc(sums_made, 1)

                    def step(g, slot, ahead, ahead_slot, ahead_turn):
                        if ahead is not None:
                            edges_and_onehot(ahead, ahead_slot, ahead_turn)
                        sum_messages(g, slot)
                        if ahead is not None:
                            fetch_q(ahead, ahead_slot, ahead_turn)

                    edges_and_onehot(0, 0, 0)
                    fetch_q(0, 0, 0)
                    with pe.Fori(0, ITERS) as i:
                        for j in range(SLOTS):
                            step(i * SLOTS + j, j, i * SLOTS + (j + 1), (j + 1) % SLOTS, i + (j + 1) // SLOTS)
                    for g in range(ITERS * SLOTS, G):
                        a = g + 1 if g + 1 < G else None
                        step(g, g % SLOTS, a, (g + 1) % SLOTS, (g + 1) // SLOTS)

                @block.scalar
                def _(act):
                    def keep_onehot(g):
                        n = pairs_of(g)
                        act.wait_ge(onehot_turned, g + 1)
                        act.copy(onehot_t[:, 0:n, :], oht_ps[:, 0:n, :]).then_inc(onehot_t_made, 1)

                    def step(g, ahead):
                        n = 2 * pairs_of(g) * H
                        act.wait_ge(score_clipped, g + 1)
                        act.activation(p_ps[:, 0:n], score_c[:, 0:n], ACT.Exp).then_inc(exp_made, 1)
                        if ahead is not None:
                            keep_onehot(ahead)

                    keep_onehot(0)
                    with act.Fori(0, ITERS) as i:
                        for j in range(SLOTS):
                            step(i * SLOTS + j, i * SLOTS + (j + 1))
                    for g in range(ITERS * SLOTS, G):
                        step(g, g + 1 if g + 1 < G else None)

                @block.vector
                def _(dve):
                    def copy_indices(g, slot):
                        dve.tensor_copy(idx[:, slot, :], src_sb[:, ds(g * T, T)]).then_inc(slot_ready, 1)

                    def make_onehot(g, slot):
                        n = 2 * pairs_of(g)
                        dve.tensor_tensor(onehot[:, slot % 2, 0:n, :],
                                          iota_ps.unsqueeze(1).to_broadcast([P, n, W]),
                                          dst_rel[:, ds(g, 1), 0:n].rearrange("p o t -> p (o t)")
                                          .unsqueeze(2).to_broadcast([P, n, W]),
                                          ALU.is_equal).then_inc(onehot_made, 1)

                    def step(g, slot, turn, ahead, next_indices):
                        n = 2 * pairs_of(g)
                        dve.wait_ge(kv_gathered[slot], 16 * T * (turn + 1) if n == T else 16 * (T * turn + n))
                        dve.wait_ge(qe_made, g + 1)
                        dve.tensor_tensor(kq[:, 0:n, :], kv[:, slot, 0:n, 0:F], qe_ps[slot % 2][:, 0:n, :],
                                          ALU.mult).then_inc(kq_made, 1)
                        dve.wait_ge(kq_made, g + 1)
                        dve.wait_ge(ee_made, g + 1)
                        dve.tensor_tensor(kqe[:, 0:n, :], kq[:, 0:n, :], ee_ps[slot % 2][:, 0:n, :],
                                          ALU.mult).then_inc(kqe_made, 1)
                        dve.wait_ge(kqe_made, g + 1)
                        dve.tensor_reduce(score[:, 0:n * H],
                                          kqe[:, 0:n, :].rearrange("p t (h d) -> p (t h) d", d=D),
                                          AX_X, ALU.add).then_inc(score_summed, 1)
                        dve.wait_ge(score_summed, g + 1)
                        dve.tensor_scalar(score_c[:, 0:n * H], score[:, 0:n * H], -CLIP, CLIP,
                                          ALU.max, ALU.min).then_inc(score_clipped, 1)
                        if ahead is not None:
                            make_onehot(ahead, (slot + 1) % SLOTS)
                        dve.wait_ge(exp_made, g + 1)
                        dve.tensor_tensor(msg[:, slot % 2, 0:n, :].rearrange("p t (h d) -> p t h d", d=D),
                                          kv[:, slot, 0:n, F:2 * F].rearrange("p t (h d) -> p t h d", d=D),
                                          p_ps[:, 0:n * H].rearrange("p (t h) -> p t h", h=H)
                                          .unsqueeze(3).to_broadcast([P, n, H, D]),
                                          ALU.mult).then_inc(msg_made, 1)
                        if next_indices is not None:
                            dve.wait_ge(msg_made, g + 1)
                            copy_indices(next_indices, slot)
                        base = dve.value_load(base_i[0:1, ds(g, 1)], min_val=0, max_val=BASE_MAX)
                        nodes = ds(base, W)
                        dve.wait_ge(sums_made, g + 1)
                        dve.tensor_tensor(acc[0:F, nodes], acc[0:F, nodes], sum_ps[0:F, slot % 2, 0:W], ALU.add)
                        dve.tensor_tensor(acc[F:2 * F, nodes], acc[F:2 * F, nodes],
                                          sum_ps[F:2 * F, slot % 2, W:2 * W], ALU.add).then_inc(acc_added, 1)
                        dve.wait_ge(acc_added, g + 1)

                    for j in range(SLOTS):
                        copy_indices(j, j)
                    make_onehot(0, 0)
                    with dve.Fori(0, ITERS) as i:
                        for j in range(SLOTS):
                            step(i * SLOTS + j, j, i, i * SLOTS + (j + 1), i * SLOTS + (SLOTS + j))
                    for g in range(ITERS * SLOTS, G):
                        step(g, g % SLOTS, g // SLOTS, g + 1 if g + 1 < G else None, None)
                    dve.tensor_scalar(iota_ps, iota_ps, float(W), None, ALU.add).then_inc(window_moved, 1)
                    dve.tensor_scalar(base_i[:, :], base_i[:, :], float(W), None, ALU.add).then_inc(window_moved, 1)
                    dve.wait_ge(window_moved, 2)

            nc.all_engine_barrier(sems_to_clear=pass_sems)

        with nc.Block() as block:
            last_banks = [ee_ps[0], ee_ps[1], qe_ps[0], qe_ps[1]]

            @block.tensor
            def _(pe):
                for c in range(CHUNKS):
                    if c >= len(last_banks):
                        pe.wait_ge(h_added, c - len(last_banks) + 1)
                    for k in range(CH):
                        mm = pe.matmul(bank(last_banks[c % 4], 512)[:, k * F:(k + 1) * F],
                                       acc[:, c * CH + k:NPAD:NT], fold[:, :], start=True, stop=True)
                    mm.then_inc(wv_turned, 1)

            @block.vector
            def _(dve):
                for c in range(CHUNKS):
                    cols = slice(c * CH, (c + 1) * CH)
                    dve.wait_ge(wv_turned, c + 1)
                    dve.tensor_tensor(h_sb[:, cols, :], bank(last_banks[c % 4], CH * F)
                                      .rearrange("p (t f) -> p t f", f=F), x_sb[:, cols, :],
                                      ALU.add).then_inc(h_added, 1)
                    dve.wait_ge(h_added, c + 1)
                    dve.tensor_reduce(mean[:, cols], h_sb[:, cols, :], AX_X, ALU.add).then_inc(mean_step, 1)
                    dve.wait_ge(mean_step, 2 * c + 1)
                    dve.tensor_scalar(neg_mean[:, cols], mean[:, cols], -1.0 / F, None, ALU.mult).then_inc(mean_step, 1)
                    dve.wait_ge(mean_step, 2 * c + 2)
                    dve.tensor_tensor(c_sb[:, cols, :], h_sb[:, cols, :],
                                      neg_mean[:, cols].unsqueeze(2).to_broadcast([P, CH, F]),
                                      ALU.add).then_inc(centered, 1)
                    if c >= 1:
                        dve.wait_ge(squared, c)
                        dve.tensor_reduce(var[:, (c - 1) * CH:c * CH], sq_sb[:, (c - 1) % 2, :, :], AX_X, ALU.add)\
                           .then_inc(var_summed, 1)
                dve.wait_ge(squared, CHUNKS)
                dve.tensor_reduce(var[:, (CHUNKS - 1) * CH:NT], sq_sb[:, (CHUNKS - 1) % 2, :, :], AX_X, ALU.add)\
                   .then_inc(var_summed, 1)
                dve.wait_ge(var_summed, CHUNKS)
                dve.tensor_scalar(var_e[:, :], var[:, :], 1.0 / F, EPS, ALU.mult, ALU.add).then_inc(std_step, 1)
                dve.wait_ge(std_rooted, 1)
                dve.reciprocal(rstd[:, :], std[:, :]).then_inc(std_step, 1)
                dve.wait_ge(std_step, 2)
                for c in range(CHUNKS):
                    cols = slice(c * CH, (c + 1) * CH)
                    dve.tensor_tensor(y_sb[:, cols, :], c_sb[:, cols, :],
                                      rstd[:, cols].unsqueeze(2).to_broadcast([P, CH, F]),
                                      ALU.mult).then_inc(y_done, 1)

            @block.scalar
            def _(act):
                for c in range(CHUNKS):
                    cols = slice(c * CH, (c + 1) * CH)
                    act.wait_ge(centered, c + 1)
                    if c >= 2:
                        act.wait_ge(var_summed, c - 1)
                    act.activation(sq_sb[:, c % 2, :, :], c_sb[:, cols, :], ACT.Square).then_inc(squared, 1)
                act.wait_ge(std_step, 1)
                act.activation(std[:, :], var_e[:, :], ACT.Sqrt).then_inc(std_rooted, 1)

            @block.sync
            def _(sp):
                for c in range(CHUNKS):
                    cols = slice(c * CH, (c + 1) * CH)
                    sp.wait_ge(y_done, c + 1)
                    sp.dma_start(out[:, cols, :], y_sb[:, cols, :]).then_inc(y_stored, 16)
                sp.wait_ge(y_stored, 16 * CHUNKS)


def kernel(x, src, dst, edge_attr_64, L0_gnn_Wq, L0_gnn_bq, L0_gnn_Wk, L0_gnn_bk, L0_gnn_We, L0_gnn_be,
           L0_gnn_Wv, L0_gnn_bv):
    import numpy as np
    import concourse.bacc as bacc
    from concourse.bass_utils import run_bass_kernel_spmd

    x, src, dst, edge_attr = (np.asarray(a) for a in (x, src, dst, edge_attr_64))
    Wq, bq, Wk, bk, We, be, Wv, bv = (np.asarray(a) for a in (
        L0_gnn_Wq, L0_gnn_bq, L0_gnn_Wk, L0_gnn_bk, L0_gnn_We, L0_gnn_be, L0_gnn_Wv, L0_gnn_bv))

    x_nodes = np.zeros((NPAD, F), x.dtype)
    x_nodes[:N] = x
    x_nodes = x_nodes.reshape(P, NT, F)
    xT = np.ascontiguousarray(x_nodes.transpose(2, 1, 0)).reshape(F, NPAD)
    xT = np.concatenate([xT, np.ones((1, NPAD), x.dtype)], 0)
    w_kvq = np.concatenate([np.concatenate([Wk.T, Wv.T, Wq.T], 1), np.concatenate([bk, bv, bq])[None]], 0)

    def by_tile(a, fill, groups):
        padded = np.full(groups * T * P, fill, a.dtype)
        padded[:E] = a
        return np.ascontiguousarray(padded.reshape(groups * T, P).T)

    src_tab = by_tile(src, 0, GPAD)
    dst_tab = by_tile(dst, N, G).reshape(P, G, T)
    dst_first = np.ascontiguousarray(np.broadcast_to(dst[::T * P][None, :], (P, G)))
    attr = np.zeros((G * T * P, F), edge_attr.dtype)
    attr[:E] = edge_attr
    attr = np.ascontiguousarray(attr.reshape(G, PAIRS, 2, P, F).transpose(0, 2, 4, 1, 3)).reshape(G, 2 * F, PAIRS * P)

    arrays = {
        "xT": xT, "x_nodes": x_nodes, "w_kvq": np.ascontiguousarray(w_kvq), "We_t": np.ascontiguousarray(We.T),
        "be_row": np.ascontiguousarray(be[None, :]), "src_tab": src_tab, "dst_tab": dst_tab,
        "dst_first": dst_first, "attr": attr,
    }
    nc = bacc.Bacc("TRN2", target_bir_lowering=False, num_devices=1)
    args = [nc.dram_tensor(name, a.shape, mybir.dt.from_np(a.dtype), kind="ExternalInput").ap()
            for name, a in arrays.items()]
    out = nc.dram_tensor("out", (P, NT, F), F32, kind="ExternalOutput").ap()
    gnn_kernel(nc, *args, out)
    r = run_bass_kernel_spmd(nc, [arrays], core_ids=[0])
    return r.results[0]["out"].reshape(NPAD, F)[:N]
```

```python
from contextlib import ExitStack

import concourse.bass as bass
from concourse import mybir

F32 = mybir.dt.float32
BF16 = mybir.dt.bfloat16
I32 = mybir.dt.int32
ALU = mybir.AluOpType
ACT = mybir.ActivationFunctionType
AX_X = mybir.AxisListType.X
ds = bass.ds

P = 128
N = 6250
E = 206250
F = 64
H = 4
D = F // H
CLIP = 5.0
EPS = 1e-5

W = 64
T = 8
PAIRS = T // 2
TILES = -(-E // P)
G = -(-TILES // T)
LAST_PAIRS = (TILES - (G - 1) * T + 1) // 2
SLOTS = 4
EARLY = 3
ITERS = (G - 1) // SLOTS
NT = -(-N // P)
NPAD = NT * P
PASSES = -(-NPAD // W)
BASE_MAX = NPAD - W
CH = 7
CHUNKS = NT // CH
OUT_COLS = [5, 8, 8, 8, 8, 8, 4]
DVE_ONES = 4
GPAD = (ITERS + 2) * SLOTS
assert CHUNKS * CH == NT and PASSES * W == NPAD and N < NPAD
HALVES = (slice(0, (NT + 1) // 2), slice((NT + 1) // 2, NT))
PE_TILES = ITERS * SLOTS // 2 - 1
PIECES = (4, 6)
assert ITERS * SLOTS < G <= GPAD and TILES % 2 == 0 and SLOTS == 4


def gnn_kernel(nc, xT, x_by_node, x_own_rows, w_kvq, We_t, be_row, src_tab, src_rows, dst_tab, dst_first, attr, out):
    ctx = ExitStack()
    with ctx:
        def sb(name, shape, dt, stack=ctx):
            return stack.enter_context(nc.sbuf_tensor(name, shape, dt))

        def ps(name, shape, dt):
            return ctx.enter_context(nc.psum_tensor(name, shape, dt))

        def sem(name):
            return ctx.enter_context(nc.semaphore(name))

        kv_table = nc.dram_tensor("kv_table", [NPAD, 2 * F], F32, kind="Internal").ap()
        q_table = nc.dram_tensor("q_table", [NPAD, 3 * F], BF16, kind="Internal").ap()

        w_sb = sb("w_sb", [P, 3 * F], F32)
        acc = sb("acc", [F, NPAD], F32)
        x_parts = sb("x_parts", [P, NT, 3, F], BF16)
        src_sb = sb("src_sb", [P, GPAD * T], I32)
        dst_neg = sb("dst_neg", [P, G, T], F32)
        base_i = sb("base_i", [P, G], I32)
        passes_i = sb("passes_i", [P, 1], I32)
        iota_w = sb("iota_w", [P, W], F32)
        ident = sb("ident", [P, P], F32)
        ident_b = sb("ident_b", [P, P], BF16)
        ones = sb("ones", [P, P], BF16)
        zero = sb("zero", [P, 1], F32)
        zero_exp = sb("zero_exp", [P, 1], F32)
        be_sb = sb("be_sb", [P, T, F], BF16)
        we_sb = sb("we_sb", [P, 2 * F], F32)
        idx = sb("idx", [P, SLOTS, T], I32)
        kv = sb("kv", [P, SLOTS, T, 2 * F], F32)
        q_win = sb("q_win", [P, SLOTS, 2, 3, F], BF16)
        xg_t_sb = sb("xg_t_sb", [P, P], F32)

        first = ExitStack()
        xT_sb = sb("xT_sb", [P, NPAD], F32, first)
        x_own = sb("x_own", [P, NT, F], F32, first)
        x_rest = sb("x_rest", [P, NT, F], F32, first)
        kv_stage = sb("kv_stage", [P, NT, 2 * F], F32, first)
        q_stage = sb("q_stage", [P, NT, 3, F], BF16, first)
        q_rest = sb("q_rest", [P, 2, CH, F], F32, first)
        be_f = sb("be_f", [P, F], F32, first)
        be_rest = sb("be_rest", [P, F], F32, first)
        be_parts = sb("be_parts", [P, 3, F], BF16, first)
        dst_i = sb("dst_i", [P, G, T], I32, first)
        first_i = sb("first_i", [P, G], I32, first)
        base_f = sb("base_f", [P, G], F32, first)
        limits = sb("limits", [P, 4], F32, first)
        limits_all = sb("limits_all", [P, 4], F32, first)
        flags = sb("flags", [P, 4], F32, first)
        general = sb("general", [P, 1], F32, first)
        minus_general = sb("minus_general", [P, 1], F32, first)
        one_pass = sb("one_pass", [P, 1], F32, first)
        iota_i = sb("iota_i", [P, W], I32, first)
        node_i = sb("node_i", [P, NT], I32, first)

        ee_ps = [ps(f"ee_ps{i}", [P, T, F], F32) for i in range(2)]
        qe_ps = ps("qe_ps", [P, T, F], F32)
        xg_bank = ps("xg_bank", [P, 4, P], F32)
        oht_ps = ps("oht_ps", [P, PAIRS, P], F32)
        sum_ps = ps("sum_ps", [P, 4, P], F32)
        node_bank = ps("node_bank", [P, 512], F32)
        exp_bank = ps("exp_bank", [P, T, F], F32)
        node_ps = node_bank[:, 0:NT]
        xg_ps = xg_bank[:].rearrange("p a b -> p (a b)")[:, 0:3 * F].rearrange("p (s f) -> p s f", s=3)
        xg_t_ps = xg_bank[0:F, 2, :]
        xg_kv_ps = xg_bank[:, 3, :]
        p_ps = exp_bank[:].rearrange("p a b -> p (a b)")[:, 0:T * H]
        kv_banks = [ee_ps[0], ee_ps[1], qe_ps, xg_bank]
        q_banks = [oht_ps, sum_ps]

        def bank(b, n):
            return b[:].rearrange("p a b -> p (a b)")[:, 0:n]

        def kv_part(c, half):
            n = 4 if half == 0 else CH - 4
            return bank(kv_banks[2 * (c % 2) + half], n * 2 * F).rearrange("p (t f) -> p t f", f=2 * F)

        w_loaded = sem("w_loaded")
        x_loaded = [sem(f"x_loaded{i}") for i in range(CHUNKS)]
        dst_loaded = sem("dst_loaded")
        src_loaded = sem("src_loaded")
        we_loaded = sem("we_loaded")
        be_loaded = sem("be_loaded")
        acc_loaded = sem("acc_loaded")
        x_own_loaded = sem("x_own_loaded")
        x_part0 = sem("x_part0")
        x_rested = sem("x_rested")
        x_part1 = sem("x_part1")
        x_part2 = sem("x_part2")
        be_step = sem("be_step")
        ident_copied = sem("ident_copied")
        ones_set = [sem("ones_set_dve"), sem("ones_set_pool")]
        zero_set = sem("zero_set")
        exp_warmed = sem("exp_warmed")
        idx_set = sem("idx_set")
        consts_zeroed = sem("consts_zeroed")
        ident_zeroed = sem("ident_zeroed")
        ident_set = sem("ident_set")
        iota_set = sem("iota_set")
        wq_scaled = sem("wq_scaled")
        kv_computed = [sem("kv_computed_a"), sem("kv_computed_b")]
        kv_staged = [sem("kv_staged_act"), sem("kv_staged_dve")]
        q_computed = sem("q_computed")
        q_part0 = sem("q_part0")
        q_rested = sem("q_rested")
        q_part1 = sem("q_part1")
        q_staged = sem("q_staged")
        kv_stored = sem("kv_stored")
        q_stored = sem("q_stored")
        dst_step = sem("dst_step")
        base_set = sem("base_set")
        rel_set = sem("rel_set")
        limits_set = sem("limits_set")
        limits_joined = sem("limits_joined")

        h_centered = sem("h_centered")
        h_turned = sem("h_turned")
        h_summed = sem("h_summed")
        mean_made = sem("mean_made")
        squared = sem("squared")
        sqrt_warmed = sem("sqrt_warmed")
        var_summed = sem("var_summed")
        eps_added = sem("eps_added")
        std_rooted = sem("std_rooted")
        rstd_made = sem("rstd_made")
        y_done = sem("y_done")
        last_done = sem("last_done")
        y_stored = sem("y_stored")

        attr_loaded = [sem(f"attr_loaded{j}") for j in range(SLOTS)]
        q_loaded = [sem(f"q_loaded{j}") for j in range(SLOTS)]
        kv_gathered = [sem(f"kv_gathered{j}") for j in range(SLOTS)]
        slot_ready = sem("slot_ready")
        gathers_begun = sem("gathers_begun")
        distance_made = sem("distance_made")
        onehot_made = sem("onehot_made")
        ee_made = sem("ee_made")
        onehot_turned = sem("onehot_turned")
        onehot_t_made = sem("onehot_t_made")
        qe_made = sem("qe_made")
        kq_made = sem("kq_made")
        kqe_made = sem("kqe_made")
        score_summed = sem("score_summed")
        score_clipped = sem("score_clipped")
        exp_made = sem("exp_made")
        msg_made = sem("msg_made")
        sums_made = sem("sums_made")
        acc_added = sem("acc_added")
        src_row_loaded = [sem(f"src_row_loaded{k}") for k in range(2)]
        src_onehot_made = sem("src_onehot_made")
        x_gathered = sem("x_gathered")
        x_kept = sem("x_kept")
        x_turned = sem("x_turned")
        x_turned_kept = sem("x_turned_kept")
        kv_projected = sem("kv_projected")
        pe_kv_made = sem("pe_kv_made")
        window_moved = sem("window_moved")
        pass_sems = range(attr_loaded[0].num, window_moved.num + 1)
        assert len(pass_sems) == 3 * SLOTS + 26

        def pairs_of(g):
            return LAST_PAIRS if isinstance(g, int) and g == G - 1 else PAIRS

        def pe_tile(g, slot):
            return slot % 2 == 1 and not (isinstance(g, int) and (g < 3 or g >= ITERS * SLOTS))

        def gathered_before(slot, turn):
            if isinstance(turn, int) and turn == 0:
                return 0
            return turn * T if slot % 2 == 0 else turn * (T - 1) + (1 if slot == 1 else 0)

        def pool_tiles(g, slot):
            return T - 1 if pe_tile(g, slot) else 2 * pairs_of(g)

        def gather(pool, g, slot):
            for t in range(pool_tiles(g, slot)):
                pool.indirect_dma_start(
                    out=kv[:, slot, t, :], out_offset=None, in_=kv_table,
                    in_offset=bass.IndirectOffsetOnAxis(ap=idx[:, slot, t:t + 1], axis=0))\
                    .then_inc(kv_gathered[slot], 16)

        def tiles_at(g):
            done, half = g // 2 - 1, g // 2
            return done if g % 2 == 0 and 0 <= done < PE_TILES else None, half if half < PE_TILES else None

        def copy_indices(dve, g, slot):
            return dve.tensor_copy(idx[:, slot, :], src_sb[:, ds(g * T, T)])

        with nc.Block() as block:
            @block.sync
            def _(sp):
                sp.dma_start(w_sb[:, :], w_kvq).then_inc(w_loaded, 16)
                for c in range(CHUNKS):
                    cols = slice(c * CH * P, (c + 1) * CH * P)
                    sp.dma_start(xT_sb[0:F, cols], xT[:, cols]).then_inc(x_loaded[c], 16)
                sp.dma_start(dst_i[:, :, :], dst_tab).then_inc(dst_loaded, 16)
                sp.dma_start(first_i[:, :], dst_first).then_inc(dst_loaded, 16)
                sp.dma_start(src_sb[:, :], src_tab).then_inc(src_loaded, 16)
                kv_rows = kv_table.rearrange("(p t) f -> p t f", t=NT)
                q_rows = q_table.rearrange("(p t) (s f) -> p t s f", t=NT, s=3)
                for c in range(CHUNKS):
                    sp.wait_ge(kv_staged[0], c + 1)
                    sp.wait_ge(kv_staged[1], c + 1)
                    sp.dma_start(kv_rows[:, c * CH:(c + 1) * CH, :],
                                 kv_stage[:, c * CH:(c + 1) * CH, :]).then_inc(kv_stored, 16)
                sp.wait_ge(consts_zeroed, 5)
                sp.dma_start(we_sb[0:F, 0:F], We_t).then_inc(we_loaded, 16)
                sp.dma_start(we_sb[F:2 * F, F:2 * F], We_t).then_inc(we_loaded, 16)
                sp.dma_start(be_f[:, :], be_row.to_broadcast([P, F])).then_inc(be_loaded, 16)
                sp.wait_ge(kv_stored, 16 * CHUNKS)
                sp.dma_start(x_own[:, :, :], x_own_rows).then_inc(x_own_loaded, 16)
                sp.dma_start(acc[:, :], x_by_node).then_inc(acc_loaded, 16)
                for c in range(CHUNKS):
                    sp.wait_ge(q_staged, c + 1)
                    sp.dma_start(q_rows[:, c * CH:(c + 1) * CH, :, :],
                                 q_stage[:, c * CH:(c + 1) * CH, :, :]).then_inc(q_stored, 16)
                sp.wait_ge(we_loaded, 16 * 2)
                sp.wait_ge(acc_loaded, 16)
                sp.wait_ge(q_stored, 16 * CHUNKS)

            @block.gpsimd
            def _(pool):
                for c in range(DVE_ONES, CHUNKS):
                    pool.memset(xT_sb[F:P, c * CH * P:(c + 1) * CH * P], 1.0).then_inc(ones_set[1], 1)
                pool.wait_ge(ones_set[1], CHUNKS - DVE_ONES)
                pool.memset(we_sb[:, :], 0.0).then_inc(consts_zeroed, 1)
                pool.memset(be_sb[:, :, :], 0.0).then_inc(consts_zeroed, 1)
                pool.memset(q_win[:, :, :, :, :], 0.0).then_inc(consts_zeroed, 1)
                pool.memset(ones[:, :], 1.0).then_inc(consts_zeroed, 1)
                pool.memset(xg_t_sb[:, :], 1.0).then_inc(consts_zeroed, 1)
                pool.memset(ident[:, :], 0.0).then_inc(ident_zeroed, 1)
                pool.wait_ge(ident_zeroed, 1)
                pool.affine_select(out=ident[:, :], in_=ident[:, :], compare_op=ALU.not_equal, fill=1.0,
                                   base=0, pattern=[[-1, P]], channel_multiplier=1).then_inc(ident_set, 1)
                pool.iota(iota_i[:, :], pattern=[[1, W]], base=0, channel_multiplier=0).then_inc(iota_set, 1)
                pool.iota(node_i[:, :], pattern=[[1, NT]], base=0, channel_multiplier=NT).then_inc(iota_set, 1)
                pool.wait_ge(idx_set, SLOTS)
                pool.wait_ge(kv_stored, 16 * CHUNKS)
                for g in range(EARLY - 1):
                    gather(pool, g, g)
                pool.wait_ge(limits_set, 4)
                pool.partition_all_reduce(limits_all[:, :], limits[:, :], P,
                                          bass.bass_isa.ReduceOp.max).then_inc(limits_joined, 1)
                gather(pool, EARLY - 1, EARLY - 1)

            @block.tensor
            def _(pe):
                pe.wait_ge(w_loaded, 16)
                for c in range(CHUNKS):
                    pe.wait_ge(x_loaded[c], 16)
                    if c < DVE_ONES:
                        pe.wait_ge(ones_set[0], c + 1)
                    else:
                        pe.wait_ge(ones_set[1], c - DVE_ONES + 1)
                    if c >= 2:
                        pe.wait_ge(kv_staged[0], c - 1)
                        pe.wait_ge(kv_staged[1], c - 1)
                    for k in range(CH):
                        t = c * CH + k
                        b = kv_banks[2 * (c % 2) + k // 4]
                        mm = pe.matmul(bank(b, 512)[:, (k % 4) * 2 * F:(k % 4 + 1) * 2 * F],
                                       xT_sb[:, t * P:(t + 1) * P], w_sb[:, 0:2 * F], start=True, stop=True)
                        if k == 3:
                            mm.then_inc(kv_computed[0], 1)
                    mm.then_inc(kv_computed[1], 1)
                pe.wait_ge(wq_scaled, 1)
                for c in range(CHUNKS):
                    if c >= 2:
                        pe.wait_ge(q_rested, c - 1)
                    for k in range(CH):
                        t = c * CH + k
                        mm = pe.matmul(bank(q_banks[c % 2], 512)[:, k * F:(k + 1) * F],
                                       xT_sb[:, t * P:(t + 1) * P], w_sb[:, 2 * F:3 * F], start=True, stop=True)
                    mm.then_inc(q_computed, 1)

            @block.scalar
            def _(act):
                act.wait_ge(zero_set, 1)
                act.activation(zero_exp[:, :], zero[:, :], ACT.Exp).then_inc(exp_warmed, 1)
                for c in range(CHUNKS):
                    act.wait_ge(kv_computed[0], c + 1)
                    act.copy(kv_stage[:, c * CH:c * CH + 4, :], kv_part(c, 0)).then_inc(kv_staged[0], 1)

                def second_part(c):
                    act.wait_ge(q_rested, c + 1)
                    act.copy(q_stage[:, c * CH:(c + 1) * CH, 1, :], q_rest[:, c % 2, :, :]).then_inc(q_part1, 1)

                for c in range(CHUNKS):
                    act.wait_ge(q_computed, c + 1)
                    act.copy(q_stage[:, c * CH:(c + 1) * CH, 0, :], bank(q_banks[c % 2], CH * F)
                             .rearrange("p (t f) -> p t f", f=F)).then_inc(q_part0, 1)
                    if c >= 1:
                        second_part(c - 1)
                second_part(CHUNKS - 1)
                act.wait_ge(x_own_loaded, 16)
                for half in HALVES:
                    act.copy(x_parts[:, half, 0, :], x_own[:, half, :]).then_inc(x_part0, 1)
                for n, half in enumerate(HALVES):
                    act.wait_ge(x_rested, n + 1)
                    act.copy(x_parts[:, half, 1, :], x_rest[:, half, :]).then_inc(x_part1, 1)

            @block.vector
            def _(dve):
                dve.memset(zero[:, :], 0.0).then_inc(zero_set, 1)
                for c in range(DVE_ONES):
                    dve.memset(xT_sb[F:P, c * CH * P:(c + 1) * CH * P], 1.0).then_inc(ones_set[0], 1)
                dve.wait_ge(w_loaded, 16)
                dve.tensor_scalar(w_sb[:, 2 * F:3 * F], w_sb[:, 2 * F:3 * F], float(D) ** -0.5, None,
                                  ALU.mult).then_inc(wq_scaled, 1)
                base_b = base_f[:, :].unsqueeze(2).to_broadcast([P, G, T])

                def check_destinations(step):
                    half = slice(step % 2 * G // 2, (step % 2 + 1) * G // 2)
                    if step < 2:
                        dve.tensor_tensor(dst_neg[:, half, :], base_b[:, half, :], dst_i[:, half, :],
                                          ALU.subtract).then_inc(rel_set, 1)
                        return
                    rel = dst_neg[:, half, :].rearrange("p g t -> p (g t)")
                    if step == 2:
                        dve.wait_ge(rel_set, 2)
                    if step < 4:
                        dve.tensor_reduce(limits[:, step - 2:step - 1], rel, AX_X, ALU.max).then_inc(limits_set, 1)
                    else:
                        dve.tensor_reduce(limits[:, step - 2:step - 1], rel, AX_X, ALU.min, negate=True)\
                           .then_inc(limits_set, 1)

                for c in range(CHUNKS):
                    dve.wait_ge(kv_computed[1], c + 1)
                    dve.tensor_copy(kv_stage[:, c * CH + 4:(c + 1) * CH, :], kv_part(c, 1)).then_inc(kv_staged[1], 1)
                    if c == 1:
                        dve.wait_ge(dst_loaded, 32)
                        dve.tensor_scalar(base_f[:, :], first_i[:, :], float(BASE_MAX), None, ALU.min)\
                           .then_inc(base_set, 1)
                        dve.wait_ge(base_set, 1)
                    elif c >= 2:
                        check_destinations(c - 2)
                dve.wait_ge(src_loaded, 16)
                for j in range(SLOTS):
                    copy_indices(dve, j, j).then_inc(idx_set, 1)
                check_destinations(5)
                dve.wait_ge(iota_set, 2)
                dve.tensor_copy(iota_w[:, :], iota_i[:, :]).then_inc(dst_step, 1)
                dve.tensor_copy(node_ps, node_i[:, :]).then_inc(dst_step, 1)
                dve.wait_ge(ident_set, 1)
                dve.tensor_copy(ident_b[:, :], ident[:, :]).then_inc(ident_copied, 1)
                def third_part(c):
                    dve.wait_ge(q_part1, c + 1)
                    dve.tensor_tensor(q_stage[:, c * CH:(c + 1) * CH, 2, :], q_rest[:, c % 2, :, :],
                                      q_stage[:, c * CH:(c + 1) * CH, 1, :], ALU.subtract).then_inc(q_staged, 1)

                for c in range(CHUNKS):
                    dve.wait_ge(q_part0, c + 1)
                    if c >= 2:
                        dve.wait_ge(q_staged, c - 1)
                    dve.tensor_tensor(q_rest[:, c % 2, :, :],
                                      bank(q_banks[c % 2], CH * F).rearrange("p (t f) -> p t f", f=F),
                                      q_stage[:, c * CH:(c + 1) * CH, 0, :], ALU.subtract).then_inc(q_rested, 1)
                    if c >= 1:
                        third_part(c - 1)
                third_part(CHUNKS - 1)
                for n, half in enumerate(HALVES):
                    dve.wait_ge(x_part0, n + 1)
                    dve.tensor_tensor(x_rest[:, half, :], x_own[:, half, :], x_parts[:, half, 0, :],
                                      ALU.subtract).then_inc(x_rested, 1)
                dve.wait_ge(be_loaded, 16)
                dve.tensor_copy(be_parts[:, 0, :], be_f[:, :]).then_inc(be_step, 1)
                dve.wait_ge(be_step, 1)
                dve.tensor_tensor(be_rest[:, :], be_f[:, :], be_parts[:, 0, :], ALU.subtract).then_inc(be_step, 1)
                dve.wait_ge(be_step, 2)
                dve.tensor_copy(be_parts[:, 1, :], be_rest[:, :]).then_inc(be_step, 1)
                dve.wait_ge(be_step, 3)
                dve.tensor_tensor(be_parts[:, 2, :], be_rest[:, :], be_parts[:, 1, :], ALU.subtract).then_inc(be_step, 1)
                dve.wait_ge(be_step, 4)
                dve.wait_ge(consts_zeroed, 5)
                for part in range(3):
                    row = slice(32 * part, 32 * part + 1)
                    dve.tensor_copy(be_sb[row, :, :], be_parts[row, part:part + 1, :].to_broadcast([1, T, F]))\
                       .then_inc(be_step, 1)
                for n, half in enumerate(HALVES):
                    dve.wait_ge(x_part1, n + 1)
                    dve.tensor_tensor(x_parts[:, half, 2, :], x_rest[:, half, :], x_parts[:, half, 1, :],
                                      ALU.subtract).then_inc(x_part2, 1)
                dve.wait_ge(limits_joined, 1)
                dve.tensor_scalar(flags[:, 0:2], limits_all[:, 0:2], 0.0, None, ALU.is_gt).then_inc(dst_step, 1)
                dve.tensor_scalar(flags[:, 2:4], limits_all[:, 2:4], float(W - 1), None, ALU.is_gt).then_inc(dst_step, 1)
                dve.wait_ge(dst_step, 4)
                dve.tensor_reduce(general[:, :], flags[:, :], AX_X, ALU.max).then_inc(dst_step, 1)
                dve.wait_ge(dst_step, 5)
                dve.tensor_scalar(one_pass[:, :], general[:, :], -1.0, 1.0, ALU.mult, ALU.add).then_inc(dst_step, 1)
                dve.tensor_scalar(minus_general[:, :], general[:, :], -1.0, None, ALU.mult).then_inc(dst_step, 1)
                dve.tensor_scalar(passes_i[:, :], general[:, :], float(PASSES - 1), 1.0, ALU.mult, ALU.add)\
                   .then_inc(dst_step, 1)
                dve.wait_ge(dst_step, 8)
                dve.tensor_scalar(base_i[:, :], base_f[:, :], one_pass[:, :], None, ALU.mult).then_inc(dst_step, 1)
                dve.scalar_tensor_tensor(out=dst_neg[:, :, :], in0=base_b, scalar=minus_general[:, :],
                                         in1=dst_neg[:, :, :], op0=ALU.mult, op1=ALU.add).then_inc(dst_step, 1)
                dve.wait_ge(dst_step, 10)
                dve.wait_ge(x_part2, 2)
                dve.wait_ge(be_step, 7)

        passes = nc.values_load(passes_i[0:1, 0:1], min_val=1, max_val=PASSES)

        first.close()
        middle = ExitStack()
        attr_sb = sb("attr_sb", [P, SLOTS, PAIRS * P], F32, middle)
        distance = sb("distance", [P, T, W], F32, middle)
        onehot = sb("onehot", [P, SLOTS, T, W], F32, middle)
        onehot_t = sb("onehot_t", [P, PAIRS, P], BF16, middle)
        kq = sb("kq", [P, T, F], F32, middle)
        kqe = sb("kqe", [P, T, F], F32, middle)
        score = sb("score", [P, T * H], F32, middle)
        score_c = sb("score_c", [P, T * H], F32, middle)
        msg = sb("msg", [P, 2, T, F], F32, middle)
        src_row = sb("src_row", [P, 2, P], I32, middle)
        src_onehot = sb("src_onehot", [P, NT, P], BF16, middle)
        xg_sb = sb("xg_sb", [P, 3, F], BF16, middle)

        with nc.Fori(0, passes) as this_pass:
            with nc.Block() as block:
                @block.sync
                def _(sp):
                    def load(g, slot):
                        n = pairs_of(g) * P
                        sp.dma_start(attr_sb[:, slot, 0:n], attr[ds(g, 1), :, 0:n].rearrange("o p n -> (o p) n"))\
                          .then_inc(attr_loaded[slot], 16)
                        base = sp.value_load(base_i[0:1, ds(g, 1)], min_val=0, max_val=BASE_MAX)
                        rows = q_table[ds(base, W), :].rearrange("n (s f) -> n s f", s=3)
                        sp.dma_start(q_win[0:W, slot, 0, :, :], rows).then_inc(q_loaded[slot], 16)
                        sp.dma_start(q_win[W:2 * W, slot, 1, :, :], rows).then_inc(q_loaded[slot], 16)

                    def load_next(g, slot):
                        sp.wait_ge(ee_made, g - SLOTS + 1)
                        sp.wait_ge(qe_made, g - SLOTS + 1)
                        load(g, slot)

                    def load_sources(g, k):
                        sp.dma_start(src_row[:, k, :], src_rows[ds(g, 1), T - 1, :].to_broadcast([P, P]))\
                          .then_inc(src_row_loaded[k], 16)

                    for k in range(2):
                        load_sources(2 * k + 3, k)
                    for j in range(SLOTS):
                        load(j, j)
                    with sp.Fori(0, ITERS - 1) as i:
                        for j in range(SLOTS):
                            load_next(i * SLOTS + (SLOTS + j), j)
                            if j >= 2:
                                sp.wait_ge(src_onehot_made, i * 4 + 2 * (j - 1))
                                load_sources(i * SLOTS + (2 * j + 3), j % 2)
                    for g in range(ITERS * SLOTS, G):
                        load_next(g, g % SLOTS)

                @block.gpsimd
                def _(pool):
                    def gather_next(g, slot):
                        pool.wait_ge(slot_ready, g - SLOTS + 1)
                        pool.sem_inc(gathers_begun, 1)
                        gather(pool, g, slot)

                    with pool.If(this_pass > 0):
                        for g in range(EARLY):
                            gather(pool, g, g)
                    for g in range(EARLY, SLOTS):
                        gather(pool, g, g)
                    with pool.Fori(0, ITERS - 1) as i:
                        for j in range(SLOTS):
                            gather_next(i * SLOTS + (SLOTS + j), j)
                    for g in range(ITERS * SLOTS, G):
                        gather_next(g, g % SLOTS)

                @block.tensor
                def _(pe):
                    def edges_and_onehot(g, slot, turn):
                        n = pairs_of(g)
                        pe.wait_ge(attr_loaded[slot], 16 * (turn + 1))
                        ee = bank(ee_ps[slot % 2], n * P)
                        pe.matmul(ee, ones[:, :], be_sb[:, 0:2 * n, :].rearrange("p t f -> p (t f)"),
                                  start=True, stop=False)
                        for k in range(n):
                            mm = pe.matmul(ee[:, k * P:(k + 1) * P], attr_sb[:, slot, k * P:(k + 1) * P],
                                           we_sb[:, :], start=False, stop=(k == n - 1))
                        mm.then_inc(ee_made, 1)
                        pe.wait_ge(onehot_made, g + 1)
                        for k in range(n):
                            mm = pe.transpose(oht_ps[:, k, :],
                                              onehot[:, slot, 2 * k:2 * k + 2, :].rearrange("p t w -> p (t w)"),
                                              ident[:, :])
                        mm.then_inc(onehot_turned, 1)

                    def fetch_q(g, slot, turn):
                        n = pairs_of(g)
                        pe.wait_ge(q_loaded[slot], 32 * (turn + 1))
                        pe.wait_ge(onehot_t_made, g + 1)
                        for k in range(n):
                            for s in range(3):
                                mm = pe.matmul(bank(qe_ps, n * P)[:, k * P:(k + 1) * P],
                                               onehot_t[:, k, :], q_win[:, slot, :, s, :],
                                               start=(s == 0), stop=(s == 2))
                        mm.then_inc(qe_made, 1)

                    def sum_messages(g, slot):
                        n = 2 * pairs_of(g)
                        pe.wait_ge(msg_made, g + 1)
                        for t in range(n):
                            mm = pe.matmul(sum_ps[0:F, slot % 2, 0:W], msg[:, slot % 2, t, :],
                                           onehot[:, slot, t, :], start=(t == 0), stop=(t == n - 1))
                        mm.then_inc(sums_made, 1)

                    def gather_half(q, half):
                        if half == 0 and not (isinstance(q, int) and q == 0):
                            pe.wait_ge(pe_kv_made, q)
                        pe.wait_ge(src_onehot_made, q * 2 + (half + 1))
                        for c in range(HALVES[half].start, HALVES[half].stop):
                            mm = pe.matmul(xg_ps, src_onehot[:, c, :], x_parts[:, c, :, :],
                                           start=(c == 0), stop=(c == NT - 1))
                        mm.then_inc(x_gathered, 1)

                    def turn_x(q):
                        pe.wait_ge(x_kept, q + 1)
                        for s in range(3):
                            mm = pe.matmul(xg_t_ps, xg_sb[:, s, :], ident_b[:, :], start=(s == 0), stop=(s == 2))
                        mm.then_inc(x_turned, 1)

                    def project(q):
                        pe.wait_ge(x_turned_kept, q + 1)
                        pe.matmul(xg_kv_ps, xg_t_sb[:, :], w_sb[:, 0:2 * F], start=True, stop=True)\
                          .then_inc(kv_projected, 1)

                    def step(g, slot, ahead, ahead_slot, ahead_turn, done_q, half_q):
                        if ahead is not None:
                            edges_and_onehot(ahead, ahead_slot, ahead_turn)
                        if done_q is not None:
                            turn_x(done_q)
                        sum_messages(g, slot)
                        if done_q is not None:
                            project(done_q)
                        if ahead is not None:
                            fetch_q(ahead, ahead_slot, ahead_turn)
                        if half_q is not None:
                            gather_half(half_q, slot % 2)

                    edges_and_onehot(0, 0, 0)
                    fetch_q(0, 0, 0)
                    for g in range(SLOTS):
                        step(g, g, g + 1, (g + 1) % SLOTS, (g + 1) // SLOTS, *tiles_at(g))
                    with pe.Fori(1, ITERS - 1) as i:
                        for j in range(SLOTS):
                            step(i * SLOTS + j, j, i * SLOTS + (j + 1), (j + 1) % SLOTS, i + (j + 1) // SLOTS,
                                 i * 2 + (j // 2 - 1) if j % 2 == 0 else None, i * 2 + j // 2)
                    for g in range((ITERS - 1) * SLOTS, G):
                        step(g, g % SLOTS, g + 1 if g + 1 < G else None, (g + 1) % SLOTS, (g + 1) // SLOTS,
                             *tiles_at(g))

                @block.scalar
                def _(act):
                    def keep_onehot(g):
                        n = pairs_of(g)
                        act.wait_ge(onehot_turned, g + 1)
                        act.copy(onehot_t[:, 0:n, :], oht_ps[:, 0:n, :]).then_inc(onehot_t_made, 1)

                    def make_onehot(g, slot):
                        n = 2 * pairs_of(g)
                        if not (isinstance(g, int) and g == 0):
                            act.wait_ge(onehot_made, g)
                        for t in range(n):
                            last = act.activation(distance[:, t, :], iota_w[:, :], ACT.Square,
                                                  bias=dst_neg[:, ds(g, 1), t:t + 1].rearrange("p o t -> p (o t)"))
                        last.then_inc(distance_made, 1)
                        act.wait_ge(distance_made, g + 1)
                        act.activation(onehot[:, slot, 0:n, :], distance[:, 0:n, :], ACT.Relu, bias=1.0, scale=-1.0)\
                           .then_inc(onehot_made, 1)

                    def step(g, slot, ahead, onehot_ahead, done_q):
                        n = 2 * pairs_of(g) * H
                        act.wait_ge(score_clipped, g + 1)
                        act.activation(p_ps[:, 0:n], score_c[:, 0:n], ACT.Exp).then_inc(exp_made, 1)
                        if done_q is not None:
                            act.wait_ge(x_gathered, done_q * 2 + 2)
                            act.copy(xg_sb[:, :, :], xg_ps).then_inc(x_kept, 1)
                        if ahead is not None:
                            keep_onehot(ahead)
                        if done_q is not None:
                            act.wait_ge(x_turned, done_q + 1)
                            act.copy(xg_t_sb[0:F, :], xg_t_ps).then_inc(x_turned_kept, 1)
                            act.wait_ge(kv_projected, done_q + 1)
                            act.copy(kv[:, slot + 1, T - 1, :], xg_kv_ps).then_inc(pe_kv_made, 1)
                        if onehot_ahead is not None:
                            make_onehot(onehot_ahead, (slot + 2) % SLOTS)

                    make_onehot(0, 0)
                    make_onehot(1, 1)
                    keep_onehot(0)
                    for g in range(SLOTS):
                        step(g, g, g + 1, g + 2, tiles_at(g)[0])
                    with act.Fori(1, ITERS - 1) as i:
                        for j in range(SLOTS):
                            step(i * SLOTS + j, j, i * SLOTS + (j + 1), i * SLOTS + (j + 2),
                                 i * 2 + (j // 2 - 1) if j % 2 == 0 else None)
                    for g in range((ITERS - 1) * SLOTS, G):
                        step(g, g % SLOTS, g + 1 if g + 1 < G else None, g + 2 if g + 2 < G else None, tiles_at(g)[0])

                @block.vector
                def _(dve):
                    def make_src_onehot(half, first, last, k):
                        cols = slice(HALVES[half].start + first, HALVES[half].start + last)
                        made = dve.tensor_tensor(src_onehot[:, cols, :],
                                                 src_row[:, k:k + 1, :].to_broadcast([P, last - first, P]),
                                                 node_ps[:, cols].unsqueeze(2).to_broadcast([P, last - first, P]),
                                                 ALU.is_equal)
                        if cols.stop == HALVES[half].stop:
                            made.then_inc(src_onehot_made, 1)

                    def add_sums(g, slot):
                        base = dve.value_load(base_i[0:1, ds(g, 1)], min_val=0, max_val=BASE_MAX)
                        nodes = ds(base, W)
                        dve.wait_ge(sums_made, g + 1)
                        if not (isinstance(g, int) and g == 0):
                            dve.wait_ge(acc_added, g)
                        dve.tensor_tensor(acc[:, nodes], acc[:, nodes], sum_ps[0:F, slot % 2, 0:W],
                                          ALU.add).then_inc(acc_added, 1)

                    def step(g, slot, turn, next_indices, half_q, k, half_turn):
                        n = 2 * pairs_of(g)
                        half = slot % 2
                        dve.wait_ge(kv_gathered[slot], 16 * (gathered_before(slot, turn) + pool_tiles(g, slot)))
                        if pe_tile(g, slot):
                            dve.wait_ge(pe_kv_made, turn * 2 + slot // 2)
                        dve.wait_ge(qe_made, g + 1)
                        dve.tensor_tensor(kq[:, 0:n, :], kv[:, slot, 0:n, 0:F], qe_ps[:, 0:n, :],
                                          ALU.mult).then_inc(kq_made, 1)
                        if not (isinstance(g, int) and g == 0):
                            add_sums(g - 1, (slot - 1) % SLOTS)
                        dve.wait_ge(kq_made, g + 1)
                        dve.wait_ge(ee_made, g + 1)
                        dve.tensor_tensor(kqe[:, 0:n, :], kq[:, 0:n, :], ee_ps[slot % 2][:, 0:n, :],
                                          ALU.mult).then_inc(kqe_made, 1)
                        if half_q is not None:
                            dve.wait_ge(src_row_loaded[k], 16 * (half_turn + 1))
                            if not (isinstance(half_q, int) and half_q == 0):
                                dve.wait_ge(x_gathered, half_q * 2 + (half - 1))
                            make_src_onehot(half, 0, PIECES[0], k)
                        dve.wait_ge(kqe_made, g + 1)
                        dve.tensor_reduce(score[:, 0:n * H],
                                          kqe[:, 0:n, :].rearrange("p t (h d) -> p (t h) d", d=D),
                                          AX_X, ALU.add).then_inc(score_summed, 1)
                        dve.wait_ge(score_summed, g + 1)
                        dve.tensor_scalar(score_c[:, 0:n * H], score[:, 0:n * H], -CLIP, CLIP,
                                          ALU.max, ALU.min).then_inc(score_clipped, 1)
                        if half_q is not None:
                            make_src_onehot(half, PIECES[0], sum(PIECES), k)
                        dve.wait_ge(exp_made, g + 1)
                        dve.tensor_tensor(msg[:, slot % 2, 0:n, :].rearrange("p t (h d) -> p t h d", d=D),
                                          kv[:, slot, 0:n, F:2 * F].rearrange("p t (h d) -> p t h d", d=D),
                                          p_ps[:, 0:n * H].rearrange("p (t h) -> p t h", h=H)
                                          .unsqueeze(3).to_broadcast([P, n, H, D]),
                                          ALU.mult).then_inc(msg_made, 1)
                        if half_q is not None:
                            make_src_onehot(half, sum(PIECES), HALVES[half].stop - HALVES[half].start, k)
                        if next_indices is not None:
                            dve.wait_ge(msg_made, g + 1)
                            copy_indices(dve, next_indices, slot).then_inc(slot_ready, 1)

                    def peeled_step(g):
                        half_q = tiles_at(g)[1]
                        step(g, g % SLOTS, g // SLOTS, g + SLOTS if g + SLOTS < G else None,
                             half_q, g // 2 % 2, half_q // 2 if half_q is not None else None)

                    for g in range(SLOTS):
                        peeled_step(g)
                    with dve.Fori(1, ITERS - 1) as i:
                        for j in range(SLOTS):
                            step(i * SLOTS + j, j, i, i * SLOTS + (SLOTS + j), i * 2 + j // 2, j // 2, i)
                    for g in range((ITERS - 1) * SLOTS, G - 1):
                        peeled_step(g)
                    last_slot = (G - 1) % SLOTS
                    dve.tensor_scalar(iota_w[:, :], iota_w[:, :], float(W), None, ALU.add).then_inc(window_moved, 1)
                    for j in range(SLOTS):
                        if j != last_slot:
                            copy_indices(dve, j, j).then_inc(window_moved, 1)
                    peeled_step(G - 1)
                    copy_indices(dve, last_slot, last_slot).then_inc(window_moved, 1)
                    add_sums(G - 1, last_slot)
                    dve.tensor_scalar(base_i[:, :], base_i[:, :], float(W), None, ALU.add).then_inc(window_moved, 1)
                    dve.wait_ge(window_moved, 2 + SLOTS)
                    dve.wait_ge(acc_added, G)

            nc.gpsimd.dma_reset(range(kv_gathered[0].num, kv_gathered[-1].num + 1))
            nc.all_engine_barrier(sems_to_clear=pass_sems)

        middle.close()
        y_sb = sb("y_sb", [P, NT, F], F32)
        c_sb = sb("c_sb", [P, NT, F], F32)
        sq_sb = sb("sq_sb", [P, 2, max(OUT_COLS), F], F32)
        h_sum = sb("h_sum", [P, NT], F32)
        neg_mean = sb("neg_mean", [P, NT], F32)
        var = sb("var", [P, NT], F32)
        var_e = sb("var_e", [P, NT], F32)
        std = sb("std", [P, NT], F32)
        rstd = sb("rstd", [P, NT], F32)

        with nc.Block() as block:
            h_banks = [ee_ps[0], ee_ps[1], qe_ps, xg_bank, oht_ps, sum_ps, exp_bank]
            assert sum(OUT_COLS) == NT and len(OUT_COLS) == len(h_banks)

            def cols_of(c):
                return slice(sum(OUT_COLS[:c]), sum(OUT_COLS[:c + 1]))

            def h_of(c):
                return bank(h_banks[c], OUT_COLS[c] * F).rearrange("p (t f) -> p t f", f=F)

            def wide(a, c):
                return a[:, cols_of(c)].unsqueeze(2).to_broadcast([P, OUT_COLS[c], F])

            last = len(OUT_COLS) - 1

            @block.tensor
            def _(pe):
                for c, n in enumerate(OUT_COLS):
                    for k in range(n):
                        mm = pe.transpose(h_of(c)[:, k, :], acc[:, cols_of(c).start + k:NPAD:NT], ident[0:F, 0:F])
                    mm.then_inc(h_turned, 1)

            @block.scalar
            def _(act):
                def root(c):
                    act.wait_ge(eps_added, c + 1)
                    act.activation(std[:, cols_of(c)], var_e[:, cols_of(c)], ACT.Sqrt).then_inc(std_rooted, 1)

                act.activation(zero_exp[:, :], zero[:, :], ACT.Sqrt).then_inc(sqrt_warmed, 1)
                for c, n in enumerate(OUT_COLS):
                    act.wait_ge(h_centered, c + 1)
                    if c >= 2:
                        act.wait_ge(var_summed, c - 1)
                    act.activation(sq_sb[:, c % 2, 0:n, :], c_sb[:, cols_of(c), :], ACT.Square).then_inc(squared, 1)
                    if c >= 1:
                        root(c - 1)
                root(last)

            @block.vector
            def _(dve):
                def sum_rows(c):
                    dve.wait_ge(h_turned, c + 1)
                    dve.tensor_reduce(h_sum[:, cols_of(c)], h_of(c), AX_X, ALU.add).then_inc(h_summed, 1)

                def mean(c):
                    dve.wait_ge(h_summed, c + 1)
                    dve.tensor_scalar(neg_mean[:, cols_of(c)], h_sum[:, cols_of(c)], -1.0 / F, None, ALU.mult)\
                       .then_inc(mean_made, 1)

                def center(c):
                    dve.wait_ge(mean_made, c + 1)
                    dve.tensor_tensor(c_sb[:, cols_of(c), :], h_of(c), wide(neg_mean, c), ALU.add)\
                       .then_inc(h_centered, 1)

                def sum_squares(c):
                    dve.wait_ge(squared, c + 1)
                    dve.tensor_reduce(var[:, cols_of(c)], sq_sb[:, c % 2, 0:OUT_COLS[c], :], AX_X, ALU.add)\
                       .then_inc(var_summed, 1)

                def add_eps(c):
                    dve.wait_ge(var_summed, c + 1)
                    dve.tensor_scalar(var_e[:, cols_of(c)], var[:, cols_of(c)], 1.0 / F, EPS, ALU.mult, ALU.add)\
                       .then_inc(eps_added, 1)

                def invert(c):
                    dve.wait_ge(std_rooted, c + 1)
                    dve.reciprocal(rstd[:, cols_of(c)], std[:, cols_of(c)]).then_inc(rstd_made, 1)

                sum_rows(0)
                mean(0)
                center(0)
                for c in range(last):
                    sum_rows(c + 1)
                    mean(c + 1)
                    if c >= 1:
                        invert(c - 1)
                    center(c + 1)
                    sum_squares(c)
                    add_eps(c)
                invert(last - 1)
                sum_squares(last)
                add_eps(last)
                invert(last)
                dve.wait_ge(rstd_made, last + 1)
                dve.tensor_tensor(y_sb[:, cols_of(last), :], c_sb[:, cols_of(last), :], wide(rstd, last),
                                  ALU.mult).then_inc(last_done, 1)

            @block.gpsimd
            def _(pool):
                for c in range(last):
                    pool.wait_ge(rstd_made, c + 1)
                    pool.tensor_tensor(y_sb[:, cols_of(c), :], c_sb[:, cols_of(c), :], wide(rstd, c),
                                       ALU.mult).then_inc(y_done, 1)

            @block.sync
            def _(sp):
                for c in range(len(OUT_COLS)):
                    if c < last:
                        sp.wait_ge(y_done, c + 1)
                    else:
                        sp.wait_ge(last_done, 1)
                    sp.dma_start(out[:, cols_of(c), :], y_sb[:, cols_of(c), :]).then_inc(y_stored, 16)
                sp.wait_ge(y_stored, 16 * len(OUT_COLS))


def kernel(x, src, dst, edge_attr_64, L0_gnn_Wq, L0_gnn_bq, L0_gnn_Wk, L0_gnn_bk, L0_gnn_We, L0_gnn_be,
           L0_gnn_Wv, L0_gnn_bv):
    import numpy as np
    import concourse.bacc as bacc
    from concourse.bass_utils import run_bass_kernel_spmd

    x, src, dst, edge_attr = (np.asarray(a) for a in (x, src, dst, edge_attr_64))
    Wq, bq, Wk, bk, We, be, Wv, bv = (np.asarray(a) for a in (
        L0_gnn_Wq, L0_gnn_bq, L0_gnn_Wk, L0_gnn_bk, L0_gnn_We, L0_gnn_be, L0_gnn_Wv, L0_gnn_bv))

    x_padded = np.zeros((NPAD, F), x.dtype)
    x_padded[:N] = x
    x_by_node = np.ascontiguousarray(x_padded.T)
    xT = np.ascontiguousarray(x_padded.reshape(P, NT, F).transpose(2, 1, 0)).reshape(F, NPAD)
    w_kvq = np.zeros((P, 3 * F), Wk.dtype)
    w_kvq[:F] = np.concatenate([Wk.T, Wv.T, Wq.T], 1)
    w_kvq[F] = np.concatenate([bk, bv, bq])

    def by_tile(a, fill, groups):
        padded = np.full(groups * T * P, fill, a.dtype)
        padded[:E] = a
        return np.ascontiguousarray(padded.reshape(groups * T, P).T)

    src_tab = by_tile(src, 0, GPAD)
    src_rows = np.ascontiguousarray(src_tab.T).reshape(GPAD, T, P)
    dst_tab = by_tile(dst, N, G).reshape(P, G, T)
    dst_first = np.ascontiguousarray(np.broadcast_to(dst[::T * P][None, :], (P, G)))
    attr = np.zeros((G * T * P, F), edge_attr.dtype)
    attr[:E] = edge_attr
    attr = np.ascontiguousarray(attr.reshape(G, PAIRS, 2, P, F).transpose(0, 2, 4, 1, 3)).reshape(G, 2 * F, PAIRS * P)

    arrays = {
        "xT": xT, "x_by_node": x_by_node, "x_own_rows": x_padded.reshape(P, NT, F), "w_kvq": w_kvq, "We_t": np.ascontiguousarray(We.T),
        "be_row": np.ascontiguousarray(be[None, :]), "src_tab": src_tab, "src_rows": src_rows, "dst_tab": dst_tab,
        "dst_first": dst_first, "attr": attr,
    }
    nc = bacc.Bacc("TRN2", target_bir_lowering=False, num_devices=1)
    args = [nc.dram_tensor(name, a.shape, mybir.dt.from_np(a.dtype), kind="ExternalInput").ap()
            for name, a in arrays.items()]
    out = nc.dram_tensor("out", (P, NT, F), F32, kind="ExternalOutput").ap()
    gnn_kernel(nc, *args, out)
    r = run_bass_kernel_spmd(nc, [arrays], core_ids=[0])
    return r.results[0]["out"].reshape(NPAD, F)[:N]
```

```python
from contextlib import ExitStack

import concourse.bass as bass
from concourse import mybir

F32 = mybir.dt.float32
BF16 = mybir.dt.bfloat16
I32 = mybir.dt.int32
ALU = mybir.AluOpType
ACT = mybir.ActivationFunctionType
AX_X = mybir.AxisListType.X
ds = bass.ds

P = 128
N = 6250
E = 206250
F = 64
H = 4
D = F // H
CLIP = 5.0
EPS = 1e-5

W = 64
T = 8
PAIRS = T // 2
TILES = -(-E // P)
G = -(-TILES // T)
LAST_PAIRS = (TILES - (G - 1) * T + 1) // 2
SLOTS = 4
EARLY = (T, T, 1)
ITERS = (G - 1) // SLOTS
NT = -(-N // P)
NPAD = NT * P
PASSES = -(-NPAD // W)
BASE_MAX = NPAD - W
CH = 7
CHUNKS = NT // CH
OUT_COLS = [5, 8, 8, 8, 8, 8, 4]
DVE_ONES = 4
GPAD = (ITERS + 2) * SLOTS
assert CHUNKS * CH == NT and PASSES * W == NPAD and N < NPAD
PE_TILES = ITERS * (SLOTS - 1) - 2
PARTS = tuple(slice(-(-NT * p // 4), -(-NT * (p + 1) // 4)) for p in range(4))
HALVES = (slice(0, (NT + 1) // 2), slice((NT + 1) // 2, NT))
PARTS_AT = (((0, 0), (0, 1), (0, 2)), ((0, 3), (1, 0), (1, 1)), ((1, 2), (1, 3), (2, 0)), ((2, 1), (2, 2), (2, 3)))
DONE_AT = (-1, None, 0, 1)
assert ITERS * SLOTS < G <= GPAD and TILES % 2 == 0 and SLOTS == 4


def gnn_kernel(nc, xT, x_own_rows, w_kvq, We_t, be_row, src_tab, dst_tab, dst_first, attr, out):
    ctx = ExitStack()
    with ctx:
        def sb(name, shape, dt, stack=ctx):
            return stack.enter_context(nc.sbuf_tensor(name, shape, dt))

        def ps(name, shape, dt):
            return ctx.enter_context(nc.psum_tensor(name, shape, dt))

        def sem(name):
            return ctx.enter_context(nc.semaphore(name))

        kv_table = nc.dram_tensor("kv_table", [NPAD, 2 * F], F32, kind="Internal").ap()
        q_table = nc.dram_tensor("q_table", [NPAD, 3 * F], BF16, kind="Internal").ap()

        w_sb = sb("w_sb", [P, 3 * F], F32)
        acc = sb("acc", [F, NPAD], F32)
        x_parts = sb("x_parts", [P, NT, 3, F], BF16)
        src_sb = sb("src_sb", [P, GPAD * T], I32)
        dst_neg = sb("dst_neg", [P, G, T], F32)
        base_i = sb("base_i", [P, G], I32)
        passes_i = sb("passes_i", [P, 1], I32)
        iota_w = sb("iota_w", [P, W], F32)
        ident = sb("ident", [P, P], F32)
        ident_b = sb("ident_b", [P, P], BF16)
        ones = sb("ones", [P, P], BF16)
        zero = sb("zero", [P, 1], F32)
        eps = sb("eps", [P, 1], F32)
        src_f = sb("src_f", [P, GPAD * T], F32)
        minus_first = sb("minus_first", [P, P], F32)
        columns = sb("columns", [P, NT, P], BF16)
        zero_exp = sb("zero_exp", [P, 1], F32)
        be_sb = sb("be_sb", [P, T, F], BF16)
        we_sb = sb("we_sb", [P, 2 * F], F32)
        idx = sb("idx", [P, SLOTS, T], I32)
        kv = sb("kv", [P, SLOTS, T, 2 * F], F32)
        q_win = sb("q_win", [P, SLOTS, 2, 3, F], BF16)
        xg_t_sb = sb("xg_t_sb", [P, P], F32)

        first = ExitStack()
        xT_sb = sb("xT_sb", [P, NPAD], F32, first)
        kv_stage = sb("kv_stage", [P, NT, 2 * F], F32, first)
        x_own, x_rest = (kv_stage[:].rearrange("p t f -> p (t f)")[:, s * NT * F:(s + 1) * NT * F]
                         .rearrange("p (t f) -> p t f", f=F) for s in range(2))
        q_stage = sb("q_stage", [P, NT, 3, F], BF16, first)
        q_rest = sb("q_rest", [P, 2, CH, F], F32, first)
        be_f = sb("be_f", [P, F], F32, first)
        be_rest = sb("be_rest", [P, F], F32, first)
        be_parts = sb("be_parts", [P, 3, F], BF16, first)
        dst_i = sb("dst_i", [P, G, T], I32, first)
        first_i = sb("first_i", [P, G], I32, first)
        base_f = sb("base_f", [P, G], F32, first)
        limits = sb("limits", [P, 4], F32, first)
        limits_all = sb("limits_all", [P, 4], F32, first)
        flags = sb("flags", [P, 4], F32, first)
        general = sb("general", [P, 1], F32, first)
        minus_general = sb("minus_general", [P, 1], F32, first)
        one_pass = sb("one_pass", [P, 1], F32, first)
        iota_i = sb("iota_i", [P, W], I32, first)
        column_i = sb("column_i", [P, NT], I32, first)
        minus_first_i = sb("minus_first_i", [P, P], I32, first)

        ee_ps = [ps(f"ee_ps{i}", [P, T, F], F32) for i in range(2)]
        qe_ps = ps("qe_ps", [P, T, F], F32)
        xg_banks = [ps(f"xg_bank{i}", [P, 4, P], F32) for i in range(2)]
        oht_bank = ps("oht_bank", [P, PAIRS, P], F32)
        oht_ps = oht_bank[:].bitcast(BF16).rearrange("p k n -> p (k n)")[:, 0:PAIRS * P]\
                            .rearrange("p (k n) -> p k n", n=P)
        sum_ps = ps("sum_ps", [P, 4, P], F32)
        src_ps = ps("src_ps", [P, 8, P], BF16)[:, 0, :]
        p_ps = sum_ps[:, 2, 0:T * H]
        xg_ps = [b[:].rearrange("p a b -> p (a b)")[:, 0:3 * F].rearrange("p (s f) -> p s f", s=3) for b in xg_banks]
        xg_t_ps = [b[0:F, 2, :] for b in xg_banks]
        xg_kv_ps = [b[:, 3, :] for b in xg_banks]
        kv_banks = [ee_ps[0], ee_ps[1], qe_ps, xg_banks[0]]
        q_banks = [oht_bank, sum_ps, xg_banks[1]]

        def bank(b, n):
            return b[:].rearrange("p a b -> p (a b)")[:, 0:n]

        def kv_part(c, half):
            n = 4 if half == 0 else CH - 4
            return bank(kv_banks[2 * (c % 2) + half], n * 2 * F).rearrange("p (t f) -> p t f", f=2 * F)

        w_loaded = sem("w_loaded")
        x_loaded = [sem(f"x_loaded{i}") for i in range(CHUNKS)]
        dst_loaded = sem("dst_loaded")
        src_loaded = sem("src_loaded")
        we_loaded = sem("we_loaded")
        be_loaded = sem("be_loaded")
        x_own_loaded = sem("x_own_loaded")
        x_part0 = sem("x_part0")
        x_rested = sem("x_rested")
        x_part1 = sem("x_part1")
        x_part2 = sem("x_part2")
        be_step = sem("be_step")
        ones_set = [sem("ones_set_dve"), sem("ones_set_pool")]
        zero_set = sem("zero_set")
        idx_set = sem("idx_set")
        consts_zeroed = sem("consts_zeroed")
        ident_zeroed = sem("ident_zeroed")
        ident_set = sem("ident_set")
        iota_set = sem("iota_set")
        column_set = sem("column_set")
        wq_scaled = sem("wq_scaled")
        kv_computed = [sem("kv_computed_a"), sem("kv_computed_b")]
        kv_staged = [sem("kv_staged_act"), sem("kv_staged_dve")]
        q_computed = sem("q_computed")
        q_part0 = sem("q_part0")
        q_rested = sem("q_rested")
        q_part1 = sem("q_part1")
        q_staged = sem("q_staged")
        kv_stored = sem("kv_stored")
        q_stored = sem("q_stored")
        dst_step = sem("dst_step")
        base_set = sem("base_set")
        rel_set = sem("rel_set")
        limits_set = sem("limits_set")
        limits_joined = sem("limits_joined")

        h_centered = sem("h_centered")
        h_turned = sem("h_turned")
        h_summed = sem("h_summed")
        squared = sem("squared")
        var_summed = sem("var_summed")
        std_rooted = sem("std_rooted")
        rstd_made = sem("rstd_made")
        y_done = sem("y_done")
        last_done = sem("last_done")
        y_stored = sem("y_stored")

        attr_loaded = [sem(f"attr_loaded{j}") for j in range(SLOTS)]
        q_loaded = [sem(f"q_loaded{j}") for j in range(SLOTS)]
        kv_gathered = [sem(f"kv_gathered{j}") for j in range(SLOTS)]
        slot_ready = sem("slot_ready")
        gathers_begun = sem("gathers_begun")
        distance_made = sem("distance_made")
        onehot_made = sem("onehot_made")
        ee_made = sem("ee_made")
        onehot_turned = sem("onehot_turned")
        onehot_t_made = sem("onehot_t_made")
        qe_made = sem("qe_made")
        kq_made = sem("kq_made")
        kqe_made = sem("kqe_made")
        score_summed = sem("score_summed")
        score_clipped = sem("score_clipped")
        exp_made = sem("exp_made")
        msg_made = sem("msg_made")
        sums_made = sem("sums_made")
        acc_added = sem("acc_added")
        src_seen_made = sem("src_seen_made")
        src_turned = sem("src_turned")
        src_onehot_made = sem("src_onehot_made")
        x_gathered = sem("x_gathered")
        x_kept = sem("x_kept")
        x_turned = sem("x_turned")
        x_turned_kept = sem("x_turned_kept")
        kv_projected = sem("kv_projected")
        pe_kv_made = sem("pe_kv_made")
        window_moved = sem("window_moved")
        pass_sems = range(attr_loaded[0].num, window_moved.num + 1)
        assert len(pass_sems) == 3 * SLOTS + 26

        def pairs_of(g):
            return LAST_PAIRS if isinstance(g, int) and g == G - 1 else PAIRS

        def pe_tile(g, slot):
            return slot != 2 and not (isinstance(g, int) and (g < 3 or g >= ITERS * SLOTS))

        def gathered_before(slot, turn):
            if isinstance(turn, int) and turn == 0:
                return 0
            if slot == 2:
                return turn * T
            return turn * (T - 1) + (1 if slot < 2 else 0)

        def pool_tiles(g, slot):
            return T - 1 if pe_tile(g, slot) else 2 * pairs_of(g)

        def gather(pool, g, slot, first=0, end=T):
            for t in range(first, min(end, pool_tiles(g, slot))):
                pool.indirect_dma_start(
                    out=kv[:, slot, t, :], out_offset=None, in_=kv_table,
                    in_offset=bass.IndirectOffsetOnAxis(ap=idx[:, slot, t:t + 1], axis=0))\
                    .then_inc(kv_gathered[slot], 16)

        def is_tile(q):
            return not isinstance(q, int) or 0 <= q < PE_TILES

        def parts_at(i, j):
            return [(i * 3 + k, k, part) for k, part in PARTS_AT[j] if is_tile(i * 3 + k)]

        def done_at(i, j):
            return i * 3 + DONE_AT[j] if DONE_AT[j] is not None and is_tile(i * 3 + DONE_AT[j]) else None

        def turned_at(i, j):
            return i * 3 + j if j >= 1 and is_tile(i * 3 + j) else None

        def seen_at(i, j):
            if j == 3 or not is_tile(i * 3 + (j + 1)):
                return None
            return i * 3 + (j + 1), i * SLOTS + (SLOTS + j + j // 2)

        def copy_indices(dve, g, slot):
            return dve.tensor_copy(idx[:, slot, :], src_sb[:, ds(g * T, T)])

        with nc.Block() as block:
            @block.sync
            def _(sp):
                sp.dma_start(w_sb[:, :], w_kvq).then_inc(w_loaded, 16)
                for c in range(CHUNKS):
                    cols = slice(c * CH * P, (c + 1) * CH * P)
                    sp.dma_start(xT_sb[0:F, cols], xT[:, cols]).then_inc(x_loaded[c], 16)
                sp.dma_start(dst_i[:, :, :], dst_tab).then_inc(dst_loaded, 16)
                sp.dma_start(first_i[:, :], dst_first).then_inc(dst_loaded, 16)
                sp.dma_start(src_sb[:, 0:SLOTS * T], src_tab[:, 0:SLOTS * T]).then_inc(src_loaded, 16)
                sp.dma_start(be_f[:, :], be_row.to_broadcast([P, F])).then_inc(be_loaded, 16)
                kv_rows = kv_table.rearrange("(p t) f -> p t f", t=NT)
                q_rows = q_table.rearrange("(p t) (s f) -> p t s f", t=NT, s=3)
                for c in range(CHUNKS):
                    sp.wait_ge(kv_staged[0], c + 1)
                    sp.wait_ge(kv_staged[1], c + 1)
                    sp.dma_start(kv_rows[:, c * CH:(c + 1) * CH, :],
                                 kv_stage[:, c * CH:(c + 1) * CH, :]).then_inc(kv_stored, 16)
                sp.wait_ge(consts_zeroed, 5)
                sp.dma_start(we_sb[0:F, 0:F], We_t).then_inc(we_loaded, 16)
                sp.dma_start(we_sb[F:2 * F, F:2 * F], We_t).then_inc(we_loaded, 16)
                sp.wait_ge(kv_stored, 16 * CHUNKS)
                sp.dma_start(x_own, x_own_rows).then_inc(x_own_loaded, 16)
                sp.dma_start(src_sb[:, SLOTS * T:], src_tab[:, SLOTS * T:]).then_inc(src_loaded, 16)
                for c in range(CHUNKS):
                    sp.wait_ge(q_staged, c + 1)
                    sp.dma_start(q_rows[:, c * CH:(c + 1) * CH, :, :],
                                 q_stage[:, c * CH:(c + 1) * CH, :, :]).then_inc(q_stored, 16)
                sp.wait_ge(we_loaded, 16 * 2)
                sp.wait_ge(q_stored, 16 * CHUNKS)

            @block.gpsimd
            def _(pool):
                pool.iota(column_i[:, :], pattern=[[1, NT]], base=0, channel_multiplier=0).then_inc(column_set, 1)
                pool.wait_ge(column_set, 1)
                for c in range(DVE_ONES, CHUNKS):
                    pool.memset(xT_sb[F:P, c * CH * P:(c + 1) * CH * P], 1.0).then_inc(ones_set[1], 1)
                pool.wait_ge(ones_set[1], CHUNKS - DVE_ONES)
                pool.memset(we_sb[:, :], 0.0).then_inc(consts_zeroed, 1)
                pool.memset(be_sb[:, :, :], 0.0).then_inc(consts_zeroed, 1)
                pool.memset(q_win[:, :, :, :, :], 0.0).then_inc(consts_zeroed, 1)
                pool.memset(ones[:, :], 1.0).then_inc(consts_zeroed, 1)
                pool.memset(xg_t_sb[:, :], 1.0).then_inc(consts_zeroed, 1)
                pool.memset(ident[:, :], 0.0).then_inc(ident_zeroed, 1)
                pool.wait_ge(ident_zeroed, 1)
                pool.affine_select(out=ident[:, :], in_=ident[:, :], compare_op=ALU.not_equal, fill=1.0,
                                   base=0, pattern=[[-1, P]], channel_multiplier=1).then_inc(ident_set, 1)
                pool.iota(iota_i[:, :], pattern=[[1, W]], base=0, channel_multiplier=0).then_inc(iota_set, 1)
                pool.iota(minus_first_i[:, :], pattern=[[-NT, P]], base=0, channel_multiplier=0).then_inc(iota_set, 1)
                pool.wait_ge(be_loaded, 16)
                pool.tensor_copy(be_parts[:, 0, :], be_f[:, :]).then_inc(be_step, 1)
                pool.wait_ge(be_step, 1)
                pool.tensor_tensor(be_rest[:, :], be_f[:, :], be_parts[:, 0, :], ALU.subtract).then_inc(be_step, 1)
                pool.wait_ge(be_step, 2)
                pool.tensor_copy(be_parts[:, 1, :], be_rest[:, :]).then_inc(be_step, 1)
                pool.wait_ge(be_step, 3)
                pool.tensor_tensor(be_parts[:, 2, :], be_rest[:, :], be_parts[:, 1, :], ALU.subtract).then_inc(be_step, 1)
                pool.wait_ge(be_step, 4)
                for part in range(3):
                    row = slice(32 * part, 32 * part + 1)
                    pool.tensor_copy(be_sb[row, :, :], be_parts[row, part:part + 1, :].to_broadcast([1, T, F]))\
                        .then_inc(be_step, 1)
                    pool.wait_ge(be_step, 5 + part)
                pool.wait_ge(idx_set, SLOTS)
                pool.wait_ge(kv_stored, 16 * CHUNKS)
                gather(pool, 0, 0, 0, EARLY[0])
                pool.wait_ge(limits_set, 4)
                pool.partition_all_reduce(limits_all[:, :], limits[:, :], P,
                                          bass.bass_isa.ReduceOp.max).then_inc(limits_joined, 1)
                for g in range(1, len(EARLY)):
                    gather(pool, g, g, 0, EARLY[g])

            @block.tensor
            def _(pe):
                pe.wait_ge(w_loaded, 16)
                for c in range(CHUNKS):
                    pe.wait_ge(x_loaded[c], 16)
                    if c < DVE_ONES:
                        pe.wait_ge(ones_set[0], c + 1)
                    else:
                        pe.wait_ge(ones_set[1], c - DVE_ONES + 1)
                    if c >= 2:
                        pe.wait_ge(kv_staged[0], c - 1)
                        pe.wait_ge(kv_staged[1], c - 1)
                    for k in range(CH):
                        t = c * CH + k
                        b = kv_banks[2 * (c % 2) + k // 4]
                        mm = pe.matmul(bank(b, 512)[:, (k % 4) * 2 * F:(k % 4 + 1) * 2 * F],
                                       xT_sb[:, t * P:(t + 1) * P], w_sb[:, 0:2 * F], start=True, stop=True)
                        if k == 3:
                            mm.then_inc(kv_computed[0], 1)
                    mm.then_inc(kv_computed[1], 1)
                pe.wait_ge(wq_scaled, 1)
                for c in range(CHUNKS):
                    if c >= len(q_banks):
                        pe.wait_ge(q_rested, c - 2)
                    for k in range(CH):
                        t = c * CH + k
                        mm = pe.matmul(bank(q_banks[c % 3], 512)[:, k * F:(k + 1) * F],
                                       xT_sb[:, t * P:(t + 1) * P], w_sb[:, 2 * F:3 * F], start=True, stop=True)
                    mm.then_inc(q_computed, 1)

            @block.scalar
            def _(act):
                def number_columns(cols):
                    n = cols.stop - cols.start
                    act.copy(columns[:, cols, :], column_i[:, cols].unsqueeze(2).to_broadcast([P, n, P]))

                act.wait_ge(zero_set, 1)
                act.activation(zero_exp[:, :], zero[:, :], ACT.Exp)
                act.wait_ge(column_set, 1)
                number_columns(HALVES[0])
                for c in range(CHUNKS):
                    act.wait_ge(kv_computed[0], c + 1)
                    act.copy(kv_stage[:, c * CH:c * CH + 4, :], kv_part(c, 0)).then_inc(kv_staged[0], 1)
                    act.wait_ge(x_loaded[c], 16)
                    act.copy(acc[:, :].rearrange("f (p t) -> f t p", t=NT)[:, c * CH:(c + 1) * CH, :],
                             xT_sb[0:F, c * CH * P:(c + 1) * CH * P].rearrange("f (t p) -> f t p", p=P))

                def second_part(c):
                    act.wait_ge(q_rested, c + 1)
                    act.copy(q_stage[:, c * CH:(c + 1) * CH, 1, :], q_rest[:, c % 2, :, :]).then_inc(q_part1, 1)

                for c in range(CHUNKS):
                    act.wait_ge(q_computed, c + 1)
                    act.copy(q_stage[:, c * CH:(c + 1) * CH, 0, :], bank(q_banks[c % 3], CH * F)
                             .rearrange("p (t f) -> p t f", f=F)).then_inc(q_part0, 1)
                    if c >= 1:
                        second_part(c - 1)
                second_part(CHUNKS - 1)
                act.wait_ge(x_own_loaded, 16)
                for half in HALVES:
                    act.copy(x_parts[:, half, 0, :], x_own[:, half, :]).then_inc(x_part0, 1)
                for n, half in enumerate(HALVES):
                    act.wait_ge(x_rested, n + 1)
                    act.copy(x_parts[:, half, 1, :], x_rest[:, half, :]).then_inc(x_part1, 1)
                act.wait_ge(src_loaded, 32)
                act.copy(src_f[:, :], src_sb[:, :])
                number_columns(HALVES[1])

            @block.vector
            def _(dve):
                dve.memset(zero[:, :], 0.0).then_inc(zero_set, 1)
                dve.memset(eps[:, :], EPS).then_inc(zero_set, 1)
                for c in range(DVE_ONES):
                    dve.memset(xT_sb[F:P, c * CH * P:(c + 1) * CH * P], 1.0).then_inc(ones_set[0], 1)
                dve.wait_ge(w_loaded, 16)
                dve.tensor_scalar(w_sb[:, 2 * F:3 * F], w_sb[:, 2 * F:3 * F], float(D) ** -0.5, None,
                                  ALU.mult).then_inc(wq_scaled, 1)
                base_b = base_f[:, :].unsqueeze(2).to_broadcast([P, G, T])

                def check_destinations(step):
                    half = slice(step % 2 * G // 2, (step % 2 + 1) * G // 2)
                    if step < 2:
                        dve.tensor_tensor(dst_neg[:, half, :], base_b[:, half, :], dst_i[:, half, :],
                                          ALU.subtract).then_inc(rel_set, 1)
                        return
                    rel = dst_neg[:, half, :].rearrange("p g t -> p (g t)")
                    if step == 2:
                        dve.wait_ge(rel_set, 2)
                    if step < 4:
                        dve.tensor_reduce(limits[:, step - 2:step - 1], rel, AX_X, ALU.max).then_inc(limits_set, 1)
                    else:
                        dve.tensor_reduce(limits[:, step - 2:step - 1], rel, AX_X, ALU.min, negate=True)\
                           .then_inc(limits_set, 1)

                for c in range(CHUNKS):
                    dve.wait_ge(kv_computed[1], c + 1)
                    dve.tensor_copy(kv_stage[:, c * CH + 4:(c + 1) * CH, :], kv_part(c, 1)).then_inc(kv_staged[1], 1)
                    if c == 1:
                        dve.wait_ge(dst_loaded, 32)
                        dve.tensor_scalar(base_f[:, :], first_i[:, :], float(BASE_MAX), None, ALU.min)\
                           .then_inc(base_set, 1)
                        dve.wait_ge(base_set, 1)
                    elif c >= 2:
                        check_destinations(c - 2)
                dve.wait_ge(src_loaded, 16)
                for j in range(SLOTS):
                    copy_indices(dve, j, j).then_inc(idx_set, 1)
                check_destinations(5)
                dve.wait_ge(iota_set, 2)
                dve.tensor_copy(iota_w[:, :], iota_i[:, :]).then_inc(dst_step, 1)
                dve.tensor_copy(minus_first[:, :], minus_first_i[:, :]).then_inc(dst_step, 1)
                dve.wait_ge(ident_set, 1)
                dve.tensor_copy(ident_b[:, :], ident[:, :])
                def third_part(c):
                    dve.wait_ge(q_part1, c + 1)
                    dve.tensor_tensor(q_stage[:, c * CH:(c + 1) * CH, 2, :], q_rest[:, c % 2, :, :],
                                      q_stage[:, c * CH:(c + 1) * CH, 1, :], ALU.subtract).then_inc(q_staged, 1)

                for c in range(CHUNKS):
                    dve.wait_ge(q_part0, c + 1)
                    if c >= 2:
                        dve.wait_ge(q_staged, c - 1)
                    dve.tensor_tensor(q_rest[:, c % 2, :, :],
                                      bank(q_banks[c % 3], CH * F).rearrange("p (t f) -> p t f", f=F),
                                      q_stage[:, c * CH:(c + 1) * CH, 0, :], ALU.subtract).then_inc(q_rested, 1)
                    if c >= 1:
                        third_part(c - 1)
                third_part(CHUNKS - 1)
                for n, half in enumerate(HALVES):
                    dve.wait_ge(x_part0, n + 1)
                    dve.tensor_tensor(x_rest[:, half, :], x_own[:, half, :], x_parts[:, half, 0, :],
                                      ALU.subtract).then_inc(x_rested, 1)
                for n, half in enumerate(HALVES):
                    dve.wait_ge(x_part1, n + 1)
                    dve.tensor_tensor(x_parts[:, half, 2, :], x_rest[:, half, :], x_parts[:, half, 1, :],
                                      ALU.subtract).then_inc(x_part2, 1)
                dve.wait_ge(limits_joined, 1)
                dve.tensor_scalar(flags[:, 0:2], limits_all[:, 0:2], 0.0, None, ALU.is_gt).then_inc(dst_step, 1)
                dve.tensor_scalar(flags[:, 2:4], limits_all[:, 2:4], float(W - 1), None, ALU.is_gt).then_inc(dst_step, 1)
                dve.wait_ge(dst_step, 4)
                dve.tensor_reduce(general[:, :], flags[:, :], AX_X, ALU.max).then_inc(dst_step, 1)
                dve.wait_ge(dst_step, 5)
                dve.tensor_scalar(one_pass[:, :], general[:, :], -1.0, 1.0, ALU.mult, ALU.add).then_inc(dst_step, 1)
                dve.tensor_scalar(minus_general[:, :], general[:, :], -1.0, None, ALU.mult).then_inc(dst_step, 1)
                dve.tensor_scalar(passes_i[:, :], general[:, :], float(PASSES - 1), 1.0, ALU.mult, ALU.add)\
                   .then_inc(dst_step, 1)
                dve.wait_ge(dst_step, 8)
                dve.tensor_scalar(base_i[:, :], base_f[:, :], one_pass[:, :], None, ALU.mult).then_inc(dst_step, 1)
                dve.scalar_tensor_tensor(out=dst_neg[:, :, :], in0=base_b, scalar=minus_general[:, :],
                                         in1=dst_neg[:, :, :], op0=ALU.mult, op1=ALU.add).then_inc(dst_step, 1)
                dve.wait_ge(dst_step, 10)
                dve.wait_ge(x_part2, 2)

        passes = nc.values_load(passes_i[0:1, 0:1], min_val=1, max_val=PASSES)

        first.close()
        middle = ExitStack()
        attr_sb = sb("attr_sb", [P, SLOTS, PAIRS * P], F32, middle)
        distance = sb("distance", [P, T, W], F32, middle)
        onehot = sb("onehot", [P, SLOTS, T, W], F32, middle)
        onehot_b = onehot[:].bitcast(BF16).rearrange("p s t (w two) -> p s (t w) two", two=2)[:, :, :, 1]\
                            .rearrange("p s (k n) -> p s k n", n=P)
        onehot_t = sb("onehot_t", [P, PAIRS, P], BF16, middle)
        kq = sb("kq", [P, T, F], F32, middle)
        kqe = sb("kqe", [P, T, F], F32, middle)
        score = sb("score", [P, T * H], F32, middle)
        score_c = sb("score_c", [P, T * H], F32, middle)
        msg = sb("msg", [P, 2, T, F], F32, middle)
        src_seen = sb("src_seen", [P, P], BF16, middle)
        src_onehot = sb("src_onehot", [P, NT, P], BF16, middle)
        xg_sb = sb("xg_sb", [P, 3, F], BF16, middle)

        with nc.Fori(0, passes) as this_pass:
            with nc.Block() as block:
                @block.sync
                def _(sp):
                    def load(g, slot):
                        n = pairs_of(g) * P
                        sp.dma_start(attr_sb[:, slot, 0:n], attr[ds(g, 1), :, 0:n].rearrange("o p n -> (o p) n"))\
                          .then_inc(attr_loaded[slot], 16)
                        base = sp.value_load(base_i[0:1, ds(g, 1)], min_val=0, max_val=BASE_MAX)
                        rows = q_table[ds(base, W), :].rearrange("n (s f) -> n s f", s=3)
                        sp.dma_start(q_win[0:W, slot, 0, :, :], rows).then_inc(q_loaded[slot], 16)
                        sp.dma_start(q_win[W:2 * W, slot, 1, :, :], rows).then_inc(q_loaded[slot], 16)

                    def load_next(g, slot):
                        sp.wait_ge(ee_made, g - SLOTS + 1)
                        sp.wait_ge(qe_made, g - SLOTS + 1)
                        load(g, slot)

                    for j in range(SLOTS):
                        load(j, j)
                    with sp.Fori(0, ITERS - 1) as i:
                        for j in range(SLOTS):
                            load_next(i * SLOTS + (SLOTS + j), j)
                    for g in range(ITERS * SLOTS, G):
                        load_next(g, g % SLOTS)

                @block.gpsimd
                def _(pool):
                    def gather_next(g, slot):
                        pool.wait_ge(slot_ready, g - SLOTS + 1)
                        pool.sem_inc(gathers_begun, 1)
                        gather(pool, g, slot)

                    with pool.If(this_pass > 0):
                        for g, tiles in enumerate(EARLY):
                            gather(pool, g, g, 0, tiles)
                    for g in range(len(EARLY) - 1, SLOTS):
                        gather(pool, g, g, EARLY[g] if g < len(EARLY) else 0)
                    with pool.Fori(0, ITERS - 1) as i:
                        for j in range(SLOTS):
                            gather_next(i * SLOTS + (SLOTS + j), j)
                    for g in range(ITERS * SLOTS, G):
                        gather_next(g, g % SLOTS)

                @block.tensor
                def _(pe):
                    def edges_and_onehot(g, slot, turn):
                        n = pairs_of(g)
                        pe.wait_ge(onehot_made, g + 1)
                        for k in range(n):
                            mm = pe.transpose(oht_ps[:, k, :], onehot_b[:, slot, k, :], ident_b[:, :])
                        mm.then_inc(onehot_turned, 1)
                        pe.wait_ge(attr_loaded[slot], 16 * (turn + 1))
                        ee = bank(ee_ps[slot % 2], n * P)
                        pe.matmul(ee, ones[:, :], be_sb[:, 0:2 * n, :].rearrange("p t f -> p (t f)"),
                                  start=True, stop=False)
                        for k in range(n):
                            mm = pe.matmul(ee[:, k * P:(k + 1) * P], attr_sb[:, slot, k * P:(k + 1) * P],
                                           we_sb[:, :], start=False, stop=(k == n - 1))
                        mm.then_inc(ee_made, 1)

                    def fetch_q(g, slot, turn):
                        n = pairs_of(g)
                        pe.wait_ge(q_loaded[slot], 32 * (turn + 1))
                        pe.wait_ge(onehot_t_made, g + 1)
                        if not (isinstance(g, int) and g == 0):
                            pe.wait_ge(kq_made, g)
                        for k in range(n):
                            for s in range(3):
                                mm = pe.matmul(bank(qe_ps, n * P)[:, k * P:(k + 1) * P],
                                               onehot_t[:, k, :], q_win[:, slot, :, s, :],
                                               start=(s == 0), stop=(s == 2))
                        mm.then_inc(qe_made, 1)

                    def sum_messages(g, slot):
                        n = 2 * pairs_of(g)
                        pe.wait_ge(msg_made, g + 1)
                        for t in range(n):
                            mm = pe.matmul(sum_ps[0:F, slot % 2, 0:W], msg[:, slot % 2, t, :],
                                           onehot[:, slot, t, :], start=(t == 0), stop=(t == n - 1))
                        mm.then_inc(sums_made, 1)

                    def turn_sources(q):
                        pe.wait_ge(src_seen_made, q + 1)
                        if not (isinstance(q, int) and q == 0):
                            pe.wait_ge(src_onehot_made, q * 4)
                        pe.transpose(src_ps, src_seen[:, :], ident_b[:, :]).then_inc(src_turned, 1)

                    def gather_part(q, k, part):
                        if part == 0:
                            before = q + (0, -2, -1)[k]
                            if not (isinstance(before, int) and before <= 0):
                                pe.wait_ge(pe_kv_made, before)
                        pe.wait_ge(src_onehot_made, q * 4 + (part + 1))
                        for c in range(PARTS[part].start, PARTS[part].stop):
                            mm = pe.matmul(xg_ps[k % 2], src_onehot[:, c, :], x_parts[:, c, :, :],
                                           start=(c == 0), stop=(c == NT - 1))
                        mm.then_inc(x_gathered, 1)

                    def turn_x(q, k):
                        pe.wait_ge(x_kept, q + 1)
                        for s in range(3):
                            mm = pe.matmul(xg_t_ps[k % 2], xg_sb[:, s, :], ident_b[:, :], start=(s == 0), stop=(s == 2))
                        mm.then_inc(x_turned, 1)

                    def project(q, k):
                        pe.wait_ge(x_turned_kept, q + 1)
                        pe.matmul(xg_kv_ps[k % 2], xg_t_sb[:, :], w_sb[:, 0:2 * F], start=True, stop=True)\
                          .then_inc(kv_projected, 1)

                    def step(g, i, j):
                        parts, done, turned = parts_at(i, j), done_at(i, j), turned_at(i, j)
                        ahead = not isinstance(g, int) or g + 1 < G
                        if ahead:
                            edges_and_onehot(g + 1, (j + 1) % SLOTS, i + (j + 1) // SLOTS)
                        if done is not None:
                            turn_x(done, DONE_AT[j] % 3)
                        early = 0 if j == 0 else 2
                        for part in parts[0:early][0:1]:
                            gather_part(*part)
                        if turned is not None and j < 3:
                            turn_sources(turned)
                        if ahead:
                            fetch_q(g + 1, (j + 1) % SLOTS, i + (j + 1) // SLOTS)
                        if done is not None:
                            project(done, DONE_AT[j] % 3)
                        for part in parts[0:early][1:2]:
                            gather_part(*part)
                        sum_messages(g, j)
                        for part in parts[early:]:
                            gather_part(*part)
                        if turned is not None and j == 3:
                            turn_sources(turned)

                    edges_and_onehot(0, 0, 0)
                    fetch_q(0, 0, 0)
                    turn_sources(0)
                    for g in range(SLOTS):
                        step(g, 0, g)
                    with pe.Fori(1, ITERS - 1) as i:
                        for j in range(SLOTS):
                            step(i * SLOTS + j, i, j)
                    for g in range((ITERS - 1) * SLOTS, G):
                        step(g, g // SLOTS, g % SLOTS)

                @block.scalar
                def _(act):
                    def keep_onehot(g):
                        n = pairs_of(g)
                        act.wait_ge(onehot_turned, g + 1)
                        act.copy(onehot_t[:, 0:n, :], oht_ps[:, 0:n, :]).then_inc(onehot_t_made, 1)

                    def make_onehot(g, slot):
                        n = 2 * pairs_of(g)
                        if not (isinstance(g, int) and g == 0):
                            act.wait_ge(onehot_made, g)
                        for t in range(n):
                            last = act.activation(distance[:, t, :], iota_w[:, :], ACT.Square,
                                                  bias=dst_neg[:, ds(g, 1), t:t + 1].rearrange("p o t -> p (o t)"))
                        last.then_inc(distance_made, 1)
                        act.wait_ge(distance_made, g + 1)
                        act.activation(onehot[:, slot, 0:n, :], distance[:, 0:n, :], ACT.Relu, bias=1.0, scale=-1.0)\
                           .then_inc(onehot_made, 1)

                    def see_sources(q, g):
                        if not (isinstance(q, int) and q == 0):
                            act.wait_ge(src_turned, q)
                        act.activation(src_seen[:, :], minus_first[:, :], ACT.Identity,
                                       bias=src_f[:, ds(g * T + (T - 1), 1)]).then_inc(src_seen_made, 1)

                    def step(g, i, j):
                        n = 2 * pairs_of(g) * H
                        done, seen = done_at(i, j), seen_at(i, j)
                        if done is not None:
                            k = DONE_AT[j] % 3
                            act.wait_ge(x_gathered, done * 4 + 4)
                            act.copy(xg_sb[:, :, :], xg_ps[k % 2]).then_inc(x_kept, 1)
                        if not isinstance(g, int) or g + 1 < G:
                            keep_onehot(g + 1)
                        if done is not None:
                            act.wait_ge(x_turned, done + 1)
                            act.copy(xg_t_sb[0:F, :], xg_t_ps[k % 2]).then_inc(x_turned_kept, 1)
                        act.wait_ge(score_clipped, g + 1)
                        act.activation(p_ps[:, 0:n], score_c[:, 0:n], ACT.Exp).then_inc(exp_made, 1)
                        if done is not None:
                            act.wait_ge(kv_projected, done + 1)
                            act.copy(kv[:, (j + 1) % SLOTS, T - 1, :], xg_kv_ps[k % 2]).then_inc(pe_kv_made, 1)
                        if not isinstance(g, int) or g + 2 < G:
                            make_onehot(g + 2, (j + 2) % SLOTS)
                        if seen is not None:
                            see_sources(*seen)

                    make_onehot(0, 0)
                    keep_onehot(0)
                    see_sources(0, 3)
                    make_onehot(1, 1)
                    for g in range(SLOTS):
                        step(g, 0, g)
                    with act.Fori(1, ITERS - 1) as i:
                        for j in range(SLOTS):
                            step(i * SLOTS + j, i, j)
                    for g in range((ITERS - 1) * SLOTS, G):
                        step(g, g // SLOTS, g % SLOTS)

                @block.vector
                def _(dve):
                    def make_src_onehot(q, k, part):
                        n = PARTS[part].stop - PARTS[part].start
                        if part == 0:
                            dve.wait_ge(src_turned, q + 1)
                        if not (isinstance(q, int) and q == 0):
                            dve.wait_ge(x_gathered, q * 4 + (part - 3))
                        dve.tensor_tensor(src_onehot[:, PARTS[part], :], src_ps.unsqueeze(1).to_broadcast([P, n, P]),
                                          columns[:, PARTS[part], :], ALU.is_equal).then_inc(src_onehot_made, 1)

                    def add_sums(g, slot):
                        base = dve.value_load(base_i[0:1, ds(g, 1)], min_val=0, max_val=BASE_MAX)
                        nodes = ds(base, W)
                        dve.wait_ge(sums_made, g + 1)
                        if not (isinstance(g, int) and g == 0):
                            dve.wait_ge(acc_added, g)
                        dve.tensor_tensor(acc[:, nodes], acc[:, nodes], sum_ps[0:F, slot % 2, 0:W],
                                          ALU.add).then_inc(acc_added, 1)

                    def step(g, i, slot):
                        n = 2 * pairs_of(g)
                        parts = parts_at(i, slot)
                        dve.wait_ge(kv_gathered[slot], 16 * (gathered_before(slot, i) + pool_tiles(g, slot)))
                        if pe_tile(g, slot):
                            dve.wait_ge(pe_kv_made, i * 3 + (-1, 0, None, 1)[slot])
                        dve.wait_ge(qe_made, g + 1)
                        dve.tensor_tensor(kq[:, 0:n, :], kv[:, slot, 0:n, 0:F], qe_ps[:, 0:n, :],
                                          ALU.mult).then_inc(kq_made, 1)
                        if not (isinstance(g, int) and g == 0):
                            add_sums(g - 1, (slot - 1) % SLOTS)
                        dve.wait_ge(kq_made, g + 1)
                        dve.wait_ge(ee_made, g + 1)
                        dve.tensor_tensor(kqe[:, 0:n, :], kq[:, 0:n, :], ee_ps[slot % 2][:, 0:n, :],
                                          ALU.mult).then_inc(kqe_made, 1)
                        for part in parts[0:1]:
                            make_src_onehot(*part)
                        dve.wait_ge(kqe_made, g + 1)
                        dve.tensor_reduce(score[:, 0:n * H],
                                          kqe[:, 0:n, :].rearrange("p t (h d) -> p (t h) d", d=D),
                                          AX_X, ALU.add).then_inc(score_summed, 1)
                        dve.wait_ge(score_summed, g + 1)
                        dve.tensor_scalar(score_c[:, 0:n * H], score[:, 0:n * H], -CLIP, CLIP,
                                          ALU.max, ALU.min).then_inc(score_clipped, 1)
                        for part in parts[1:2]:
                            make_src_onehot(*part)
                        dve.wait_ge(exp_made, g + 1)
                        dve.tensor_tensor(msg[:, slot % 2, 0:n, :].rearrange("p t (h d) -> p t h d", d=D),
                                          kv[:, slot, 0:n, F:2 * F].rearrange("p t (h d) -> p t h d", d=D),
                                          p_ps[:, 0:n * H].rearrange("p (t h) -> p t h", h=H)
                                          .unsqueeze(3).to_broadcast([P, n, H, D]),
                                          ALU.mult).then_inc(msg_made, 1)
                        for part in parts[2:3]:
                            make_src_onehot(*part)
                        if not isinstance(g, int) or g + SLOTS < G:
                            dve.wait_ge(msg_made, g + 1)
                            copy_indices(dve, g + SLOTS, slot).then_inc(slot_ready, 1)

                    for g in range(SLOTS):
                        step(g, 0, g)
                    with dve.Fori(1, ITERS - 1) as i:
                        for j in range(SLOTS):
                            step(i * SLOTS + j, i, j)
                    for g in range((ITERS - 1) * SLOTS, G - 1):
                        step(g, g // SLOTS, g % SLOTS)
                    last_slot = (G - 1) % SLOTS
                    dve.tensor_scalar(iota_w[:, :], iota_w[:, :], float(W), None, ALU.add).then_inc(window_moved, 1)
                    for j in range(SLOTS):
                        if j != last_slot:
                            copy_indices(dve, j, j).then_inc(window_moved, 1)
                    step(G - 1, (G - 1) // SLOTS, last_slot)
                    copy_indices(dve, last_slot, last_slot).then_inc(window_moved, 1)
                    add_sums(G - 1, last_slot)
                    dve.tensor_scalar(base_i[:, :], base_i[:, :], float(W), None, ALU.add).then_inc(window_moved, 1)
                    dve.wait_ge(window_moved, 2 + SLOTS)
                    dve.wait_ge(acc_added, G)

            nc.gpsimd.dma_reset(range(kv_gathered[0].num, kv_gathered[-1].num + 1))
            nc.all_engine_barrier(sems_to_clear=pass_sems)

        middle.close()
        y_sb = sb("y_sb", [P, NT, F], F32)
        c_sb = sb("c_sb", [P, NT, F], F32)
        sq_sb = sb("sq_sb", [P, 2, max(OUT_COLS), F], F32)
        h_sum = sb("h_sum", [P, NT], F32)
        var = sb("var", [P, NT], F32)
        std = sb("std", [P, NT], F32)
        rstd = sb("rstd", [P, NT], F32)

        with nc.Block() as block:
            h_banks = [ee_ps[0], ee_ps[1], qe_ps, xg_banks[0], xg_banks[1], oht_bank, sum_ps]
            assert sum(OUT_COLS) == NT and len(OUT_COLS) == len(h_banks)

            def cols_of(c):
                return slice(sum(OUT_COLS[:c]), sum(OUT_COLS[:c + 1]))

            def h_of(c):
                return bank(h_banks[c], OUT_COLS[c] * F).rearrange("p (t f) -> p t f", f=F)

            def wide(a, c):
                return a[:, cols_of(c)].unsqueeze(2).to_broadcast([P, OUT_COLS[c], F])

            last = len(OUT_COLS) - 1

            @block.tensor
            def _(pe):
                for c, n in enumerate(OUT_COLS):
                    for k in range(n):
                        mm = pe.transpose(h_of(c)[:, k, :], acc[:, cols_of(c).start + k:NPAD:NT], ident[0:F, 0:F])
                    mm.then_inc(h_turned, 1)

            @block.scalar
            def _(act):
                def root(c):
                    act.wait_ge(var_summed, c + 1)
                    act.activation(std[:, cols_of(c)], var[:, cols_of(c)], ACT.Sqrt, bias=eps[:, :], scale=1.0 / F)\
                       .then_inc(std_rooted, 1)

                act.activation(zero_exp[:, :], zero[:, :], ACT.Sqrt)
                for c, n in enumerate(OUT_COLS):
                    act.wait_ge(h_centered, c + 1)
                    if c >= 2:
                        act.wait_ge(var_summed, c - 1)
                    act.activation(sq_sb[:, c % 2, 0:n, :], c_sb[:, cols_of(c), :], ACT.Square).then_inc(squared, 1)
                    if c >= 1:
                        root(c - 1)
                root(last)

            @block.vector
            def _(dve):
                def sum_rows(c):
                    dve.wait_ge(h_turned, c + 1)
                    dve.tensor_reduce(h_sum[:, cols_of(c)], h_of(c), AX_X, ALU.add).then_inc(h_summed, 1)

                def center(c):
                    dve.wait_ge(h_summed, c + 1)
                    dve.scalar_tensor_tensor(out=c_sb[:, cols_of(c), :], in0=wide(h_sum, c), scalar=-1.0 / F,
                                             in1=h_of(c), op0=ALU.mult, op1=ALU.add).then_inc(h_centered, 1)

                def sum_squares(c):
                    dve.wait_ge(squared, c + 1)
                    dve.tensor_reduce(var[:, cols_of(c)], sq_sb[:, c % 2, 0:OUT_COLS[c], :], AX_X, ALU.add)\
                       .then_inc(var_summed, 1)

                def invert(c):
                    dve.wait_ge(std_rooted, c + 1)
                    dve.reciprocal(rstd[:, cols_of(c)], std[:, cols_of(c)]).then_inc(rstd_made, 1)

                sum_rows(0)
                sum_rows(1)
                center(0)
                for c in range(last):
                    center(c + 1)
                    if c + 2 <= last:
                        sum_rows(c + 2)
                    if c >= 1:
                        invert(c - 1)
                    sum_squares(c)
                invert(last - 1)
                sum_squares(last)
                invert(last)
                dve.wait_ge(rstd_made, last + 1)
                dve.tensor_tensor(y_sb[:, cols_of(last), :], c_sb[:, cols_of(last), :], wide(rstd, last),
                                  ALU.mult).then_inc(last_done, 1)

            @block.gpsimd
            def _(pool):
                for c in range(last):
                    pool.wait_ge(rstd_made, c + 1)
                    pool.tensor_tensor(y_sb[:, cols_of(c), :], c_sb[:, cols_of(c), :], wide(rstd, c),
                                       ALU.mult).then_inc(y_done, 1)

            @block.sync
            def _(sp):
                for c in range(len(OUT_COLS)):
                    if c < last:
                        sp.wait_ge(y_done, c + 1)
                    else:
                        sp.wait_ge(last_done, 1)
                    sp.dma_start(out[:, cols_of(c), :], y_sb[:, cols_of(c), :]).then_inc(y_stored, 16)
                sp.wait_ge(y_stored, 16 * len(OUT_COLS))


def kernel(x, src, dst, edge_attr_64, L0_gnn_Wq, L0_gnn_bq, L0_gnn_Wk, L0_gnn_bk, L0_gnn_We, L0_gnn_be,
           L0_gnn_Wv, L0_gnn_bv):
    import numpy as np
    import concourse.bacc as bacc
    from concourse.bass_utils import run_bass_kernel_spmd

    x, src, dst, edge_attr = (np.asarray(a) for a in (x, src, dst, edge_attr_64))
    Wq, bq, Wk, bk, We, be, Wv, bv = (np.asarray(a) for a in (
        L0_gnn_Wq, L0_gnn_bq, L0_gnn_Wk, L0_gnn_bk, L0_gnn_We, L0_gnn_be, L0_gnn_Wv, L0_gnn_bv))

    x_padded = np.zeros((NPAD, F), x.dtype)
    x_padded[:N] = x
    xT = np.ascontiguousarray(x_padded.reshape(P, NT, F).transpose(2, 1, 0)).reshape(F, NPAD)
    w_kvq = np.zeros((P, 3 * F), Wk.dtype)
    w_kvq[:F] = np.concatenate([Wk.T, Wv.T, Wq.T], 1)
    w_kvq[F] = np.concatenate([bk, bv, bq])

    def by_tile(a, fill, groups):
        padded = np.full(groups * T * P, fill, a.dtype)
        padded[:E] = a
        return np.ascontiguousarray(padded.reshape(groups * T, P).T)

    src_tab = by_tile(src, 0, GPAD)
    dst_tab = by_tile(dst, N, G).reshape(P, G, T)
    dst_first = np.ascontiguousarray(np.broadcast_to(dst[::T * P][None, :], (P, G)))
    attr = np.zeros((G * T * P, F), edge_attr.dtype)
    attr[:E] = edge_attr
    attr = np.ascontiguousarray(attr.reshape(G, PAIRS, 2, P, F).transpose(0, 2, 4, 1, 3)).reshape(G, 2 * F, PAIRS * P)

    arrays = {
        "xT": xT, "x_own_rows": x_padded.reshape(P, NT, F), "w_kvq": w_kvq, "We_t": np.ascontiguousarray(We.T),
        "be_row": np.ascontiguousarray(be[None, :]), "src_tab": src_tab, "dst_tab": dst_tab,
        "dst_first": dst_first, "attr": attr,
    }
    nc = bacc.Bacc("TRN2", target_bir_lowering=False, num_devices=1)
    args = [nc.dram_tensor(name, a.shape, mybir.dt.from_np(a.dtype), kind="ExternalInput").ap()
            for name, a in arrays.items()]
    out = nc.dram_tensor("out", (P, NT, F), F32, kind="ExternalOutput").ap()
    gnn_kernel(nc, *args, out)
    r = run_bass_kernel_spmd(nc, [arrays], core_ids=[0])
    return r.results[0]["out"].reshape(NPAD, F)[:N]
```
